# Optimizing a Trainium2 kernel written in Bass

```python
import numpy as np
import jax
import jax.numpy as jnp

def _softmax(x, axis=-1):
    return jax.nn.softmax(x, axis=axis)

def _gelu(x):
    return jax.nn.gelu(x, approximate=True)

def _silu(x):
    return jax.nn.silu(x)

def _sigmoid(x):
    return jax.nn.sigmoid(x)

def _layernorm(x, axis=-1, eps=1e-05):
    m = jnp.mean(x, axis=axis, keepdims=True)
    v = jnp.var(x, axis=axis, keepdims=True)
    return (x - m) / jnp.sqrt(v + eps)

def _scatter_add(tgt, idx, src, axis=0):
    return tgt.at[idx].add(src)

def _segment_sum(src, seg, n):
    return jax.ops.segment_sum(src, seg, n)
kernel_name = 'mk_adaln_ffn_d4_seqx_r8_621cd3'

def setup_inputs(seed: int=0):
    np.random.seed(seed)
    _w = jnp.asarray

    def _rec_inputs():
        import jax
        import jax.numpy as jnp
        _rk = jax.random.key(seed)
        x = -0.000125 + 0.9999 * jax.random.normal(jax.random.fold_in(_rk, 1), (4, 256, 256), jnp.float32)
        _lenS = 256 - jax.random.randint(jax.random.fold_in(_rk, 7), (4,), 0, max(1, 256 // 4) + 1, jnp.int32)
        _lenS2 = 256 - jax.random.randint(jax.random.fold_in(_rk, 8), (4,), 0, max(1, 256 // 4) + 1, jnp.int32)
        fside_BxSxS_0 = -1.52775e-05 + 0.999936 * jax.random.normal(jax.random.fold_in(_rk, 11), (4, 256, 256), jnp.float32)
        cond_512 = -5.03954e-05 + 1.00559 * jax.random.normal(jax.random.fold_in(_rk, 12), (4, 64), jnp.float32)
        return (x, fside_BxSxS_0, cond_512)
    x, fside_BxSxS_0, cond_512 = _rec_inputs()

    def _L0_cond_setup():
        import jax, jax.numpy as jnp
        from jax import lax
        import numpy as np
        B, T, C, TD = (8, 256, 256, 64)

        def _bi_wkv(r, k, v, w, u, time_emb):
            tf = jax.nn.sigmoid(jnp.sum(time_emb, axis=-1))[:, None, None]
            decay = jnp.exp(-jnp.exp(w.astype(jnp.float32)))[None, :] * (0.5 + 0.5 * tf[:, :, 0])
            kf = k.astype(jnp.float32)
            vf = v.astype(jnp.float32)
            ek = jnp.exp(jnp.minimum(kf, 30.0))
            ekv = ek * vf

            def step(carry, x):
                a, b = carry
                ekv_t, ek_t = x
                a = a * decay + ekv_t
                b = b * decay + ek_t
                return ((a, b), (a, b))
            ekv_t = jnp.swapaxes(ekv, 0, 1)
            ek_t = jnp.swapaxes(ek, 0, 1)
            init = (jnp.zeros_like(decay), jnp.zeros_like(decay))
            _, (nf, df) = lax.scan(step, init, (ekv_t, ek_t))
            _, (nb, db) = lax.scan(step, init, (ekv_t, ek_t), reverse=True)
            nf = jnp.swapaxes(nf, 0, 1)
            df = jnp.swapaxes(df, 0, 1)
            nb = jnp.swapaxes(nb, 0, 1)
            db = jnp.swapaxes(db, 0, 1)
            euk = jnp.exp(jnp.minimum(u.astype(jnp.float32)[None, None, :] + kf, 30.0))
            num = nf + nb - ekv + euk * vf
            den = df + db - ek + euk
            base = jax.nn.sigmoid(r.astype(jnp.float32)) * (num / jnp.maximum(den, 1e-08))
            out = base * (0.8 + 0.2 * tf)
            return out.astype(r.dtype)
        key = jax.random.key(seed)
        ks = jax.random.split(key, 6)
        return {'r': jax.random.normal(ks[0], (B, T, C), dtype=jnp.float32), 'k': jax.random.normal(ks[1], (B, T, C), dtype=jnp.float32), 'v': jax.random.normal(ks[2], (B, T, C), dtype=jnp.float32), 'w': jax.random.normal(ks[3], (C,), dtype=jnp.float32), 'u': jax.random.normal(ks[4], (C,), dtype=jnp.float32), 'time_emb': jax.random.normal(ks[5], (B, TD), dtype=jnp.float32)}
    _L0_cond_all = _L0_cond_setup()
    _L0_cond_in = {k: v for k, v in _L0_cond_all.items() if k in ('w', 'u')}
    del _L0_cond_all

    def _L0_ffn_setup():
        import jax, jax.numpy as jnp
        import numpy as np
        NUM_EXPERTS = 128
        NUM_KEPT = 48
        TOP_K = 8
        HIDDEN = 256
        INTER = 96
        CAP = 96
        BATCH, SEQ = (2, 128)
        key = jax.random.key(seed)
        k1, k2, k3, k4 = jax.random.split(key, 4)
        hidden_states = jax.random.normal(k1, (BATCH, SEQ, HIDDEN), jnp.float32)
        gate_weight = jax.random.normal(k2, (NUM_EXPERTS, HIDDEN), jnp.float32) * 0.02
        gate_up_proj = jax.random.normal(k3, (NUM_KEPT, 2 * INTER, HIDDEN), jnp.float32) * 0.02
        down_proj = jax.random.normal(k4, (NUM_KEPT, HIDDEN, INTER), jnp.float32) * 0.02
        o2n = -np.ones(NUM_EXPERTS, np.int32)
        o2n[np.arange(NUM_KEPT) * 2] = np.arange(NUM_KEPT, dtype=np.int32)
        old_to_new = jnp.asarray(o2n)
        return {'hidden_states': hidden_states, 'gate_weight': gate_weight, 'gate_up_proj': gate_up_proj, 'down_proj': down_proj, 'old_to_new': old_to_new}
    _L0_ffn_all = _L0_ffn_setup()
    _L0_ffn_in = {k: v for k, v in _L0_ffn_all.items() if k in ('gate_weight', 'gate_up_proj', 'down_proj', 'old_to_new')}
    del _L0_ffn_all

    def _L1_cond_setup():
        import jax, jax.numpy as jnp
        from jax import lax
        import numpy as np
        B, T, C, TD = (8, 256, 256, 64)

        def _bi_wkv(r, k, v, w, u, time_emb):
            tf = jax.nn.sigmoid(jnp.sum(time_emb, axis=-1))[:, None, None]
            decay = jnp.exp(-jnp.exp(w.astype(jnp.float32)))[None, :] * (0.5 + 0.5 * tf[:, :, 0])
            kf = k.astype(jnp.float32)
            vf = v.astype(jnp.float32)
            ek = jnp.exp(jnp.minimum(kf, 30.0))
            ekv = ek * vf

            def step(carry, x):
                a, b = carry
                ekv_t, ek_t = x
                a = a * decay + ekv_t
                b = b * decay + ek_t
                return ((a, b), (a, b))
            ekv_t = jnp.swapaxes(ekv, 0, 1)
            ek_t = jnp.swapaxes(ek, 0, 1)
            init = (jnp.zeros_like(decay), jnp.zeros_like(decay))
            _, (nf, df) = lax.scan(step, init, (ekv_t, ek_t))
            _, (nb, db) = lax.scan(step, init, (ekv_t, ek_t), reverse=True)
            nf = jnp.swapaxes(nf, 0, 1)
            df = jnp.swapaxes(df, 0, 1)
            nb = jnp.swapaxes(nb, 0, 1)
            db = jnp.swapaxes(db, 0, 1)
            euk = jnp.exp(jnp.minimum(u.astype(jnp.float32)[None, None, :] + kf, 30.0))
            num = nf + nb - ekv + euk * vf
            den = df + db - ek + euk
            base = jax.nn.sigmoid(r.astype(jnp.float32)) * (num / jnp.maximum(den, 1e-08))
            out = base * (0.8 + 0.2 * tf)
            return out.astype(r.dtype)
        key = jax.random.key(seed)
        ks = jax.random.split(key, 6)
        return {'r': jax.random.normal(ks[0], (B, T, C), dtype=jnp.float32), 'k': jax.random.normal(ks[1], (B, T, C), dtype=jnp.float32), 'v': jax.random.normal(ks[2], (B, T, C), dtype=jnp.float32), 'w': jax.random.normal(ks[3], (C,), dtype=jnp.float32), 'u': jax.random.normal(ks[4], (C,), dtype=jnp.float32), 'time_emb': jax.random.normal(ks[5], (B, TD), dtype=jnp.float32)}
    _L1_cond_all = _L1_cond_setup()
    _L1_cond_in = {k: v for k, v in _L1_cond_all.items() if k in ('w', 'u')}
    del _L1_cond_all

    def _L1_ffn_setup():
        import jax, jax.numpy as jnp
        import numpy as np
        from jax import lax
        E = 8
        K = 2
        D = 256
        H = 176
        NS = 2
        B, T = (2, 256)
        EPS = 1e-20
        HS = H * NS

        def _silu(v):
            return v * jax.nn.sigmoid(v)
        key = jax.random.key(seed)
        ks = jax.random.split(key, 8)
        s = 0.02
        return {'x': jax.random.normal(ks[0], (B, T, D), jnp.float32), 'router_w': jax.random.normal(ks[1], (E, D), jnp.float32) * 0.006, 'wg': jax.random.normal(ks[2], (E, D, H), jnp.float32) * s, 'wu': jax.random.normal(ks[3], (E, D, H), jnp.float32) * s, 'wd': jax.random.normal(ks[4], (E, H, D), jnp.float32) * s, 'sg': jax.random.normal(ks[5], (D, HS), jnp.float32) * s, 'su': jax.random.normal(ks[6], (D, HS), jnp.float32) * s, 'sd': jax.random.normal(ks[7], (HS, D), jnp.float32) * s}
    _L1_ffn_all = _L1_ffn_setup()
    _L1_ffn_in = {k: v for k, v in _L1_ffn_all.items() if k in ('router_w', 'wg', 'wu', 'wd', 'sg', 'su', 'sd')}
    del _L1_ffn_all

    def _L2_cond_setup():
        import jax, jax.numpy as jnp
        from jax import lax
        import numpy as np
        B, T, C, TD = (8, 256, 256, 64)

        def _bi_wkv(r, k, v, w, u, time_emb):
            tf = jax.nn.sigmoid(jnp.sum(time_emb, axis=-1))[:, None, None]
            decay = jnp.exp(-jnp.exp(w.astype(jnp.float32)))[None, :] * (0.5 + 0.5 * tf[:, :, 0])
            kf = k.astype(jnp.float32)
            vf = v.astype(jnp.float32)
            ek = jnp.exp(jnp.minimum(kf, 30.0))
            ekv = ek * vf

            def step(carry, x):
                a, b = carry
                ekv_t, ek_t = x
                a = a * decay + ekv_t
                b = b * decay + ek_t
                return ((a, b), (a, b))
            ekv_t = jnp.swapaxes(ekv, 0, 1)
            ek_t = jnp.swapaxes(ek, 0, 1)
            init = (jnp.zeros_like(decay), jnp.zeros_like(decay))
            _, (nf, df) = lax.scan(step, init, (ekv_t, ek_t))
            _, (nb, db) = lax.scan(step, init, (ekv_t, ek_t), reverse=True)
            nf = jnp.swapaxes(nf, 0, 1)
            df = jnp.swapaxes(df, 0, 1)
            nb = jnp.swapaxes(nb, 0, 1)
            db = jnp.swapaxes(db, 0, 1)
            euk = jnp.exp(jnp.minimum(u.astype(jnp.float32)[None, None, :] + kf, 30.0))
            num = nf + nb - ekv + euk * vf
            den = df + db - ek + euk
            base = jax.nn.sigmoid(r.astype(jnp.float32)) * (num / jnp.maximum(den, 1e-08))
            out = base * (0.8 + 0.2 * tf)
            return out.astype(r.dtype)
        key = jax.random.key(seed)
        ks = jax.random.split(key, 6)
        return {'r': jax.random.normal(ks[0], (B, T, C), dtype=jnp.float32), 'k': jax.random.normal(ks[1], (B, T, C), dtype=jnp.float32), 'v': jax.random.normal(ks[2], (B, T, C), dtype=jnp.float32), 'w': jax.random.normal(ks[3], (C,), dtype=jnp.float32), 'u': jax.random.normal(ks[4], (C,), dtype=jnp.float32), 'time_emb': jax.random.normal(ks[5], (B, TD), dtype=jnp.float32)}
    _L2_cond_all = _L2_cond_setup()
    _L2_cond_in = {k: v for k, v in _L2_cond_all.items() if k in ('w', 'u')}
    del _L2_cond_all

    def _L2_ffn_setup():
        import jax, jax.numpy as jnp
        import numpy as np
        TOPK = 2
        HID, INTER, E, SHARED_INTER = (256, 176, 14, 352)
        key = jax.random.key(seed)
        ks = jax.random.split(key, 11)
        s = 0.02
        return {'x': jax.random.normal(ks[0], (4, 64, HID), jnp.float32), 'gate_w': jax.random.normal(ks[1], (E, HID), jnp.float32) * s, 'cls_w': jax.random.normal(ks[2], (E, HID), jnp.float32) * s, 'extra_scale': jax.random.normal(ks[3], (E,), jnp.float32) * 0.1, 'extra_bias': jax.random.normal(ks[4], (E,), jnp.float32) * 0.01, 'wg': jax.random.normal(ks[5], (E, INTER, HID), jnp.float32) * s, 'wu': jax.random.normal(ks[6], (E, INTER, HID), jnp.float32) * s, 'wd': jax.random.normal(ks[7], (E, HID, INTER), jnp.float32) * s, 'sg': jax.random.normal(ks[8], (SHARED_INTER, HID), jnp.float32) * s, 'su': jax.random.normal(ks[9], (SHARED_INTER, HID), jnp.float32) * s, 'sd': jax.random.normal(ks[10], (HID, SHARED_INTER), jnp.float32) * s}
    _L2_ffn_all = _L2_ffn_setup()
    _L2_ffn_in = {k: v for k, v in _L2_ffn_all.items() if k in ('gate_w', 'cls_w', 'extra_scale', 'extra_bias', 'wg', 'wu', 'wd', 'sg', 'su', 'sd')}
    del _L2_ffn_all

    def _L3_cond_setup():
        import jax, jax.numpy as jnp
        from jax import lax
        import numpy as np
        B, T, C, TD = (8, 256, 256, 64)

        def _bi_wkv(r, k, v, w, u, time_emb):
            tf = jax.nn.sigmoid(jnp.sum(time_emb, axis=-1))[:, None, None]
            decay = jnp.exp(-jnp.exp(w.astype(jnp.float32)))[None, :] * (0.5 + 0.5 * tf[:, :, 0])
            kf = k.astype(jnp.float32)
            vf = v.astype(jnp.float32)
            ek = jnp.exp(jnp.minimum(kf, 30.0))
            ekv = ek * vf

            def step(carry, x):
                a, b = carry
                ekv_t, ek_t = x
                a = a * decay + ekv_t
                b = b * decay + ek_t
                return ((a, b), (a, b))
            ekv_t = jnp.swapaxes(ekv, 0, 1)
            ek_t = jnp.swapaxes(ek, 0, 1)
            init = (jnp.zeros_like(decay), jnp.zeros_like(decay))
            _, (nf, df) = lax.scan(step, init, (ekv_t, ek_t))
            _, (nb, db) = lax.scan(step, init, (ekv_t, ek_t), reverse=True)
            nf = jnp.swapaxes(nf, 0, 1)
            df = jnp.swapaxes(df, 0, 1)
            nb = jnp.swapaxes(nb, 0, 1)
            db = jnp.swapaxes(db, 0, 1)
            euk = jnp.exp(jnp.minimum(u.astype(jnp.float32)[None, None, :] + kf, 30.0))
            num = nf + nb - ekv + euk * vf
            den = df + db - ek + euk
            base = jax.nn.sigmoid(r.astype(jnp.float32)) * (num / jnp.maximum(den, 1e-08))
            out = base * (0.8 + 0.2 * tf)
            return out.astype(r.dtype)
        key = jax.random.key(seed)
        ks = jax.random.split(key, 6)
        return {'r': jax.random.normal(ks[0], (B, T, C), dtype=jnp.float32), 'k': jax.random.normal(ks[1], (B, T, C), dtype=jnp.float32), 'v': jax.random.normal(ks[2], (B, T, C), dtype=jnp.float32), 'w': jax.random.normal(ks[3], (C,), dtype=jnp.float32), 'u': jax.random.normal(ks[4], (C,), dtype=jnp.float32), 'time_emb': jax.random.normal(ks[5], (B, TD), dtype=jnp.float32)}
    _L3_cond_all = _L3_cond_setup()
    _L3_cond_in = {k: v for k, v in _L3_cond_all.items() if k in ('w', 'u')}
    del _L3_cond_all

    def _L3_ffn_setup():
        import jax, jax.numpy as jnp
        import numpy as np
        E, TOP_K, H, I = (16, 2, 256, 128)
        B, S = (2, 256)
        GROUP = 16
        RSF = 1.0

        def _dequant(q, blocks_scale, global_scale):
            e, k, n = q.shape
            w = (q.astype(jnp.float32) - 8.0).reshape(e, k // GROUP, GROUP, n)
            w = w * blocks_scale[:, :, None, :]
            return w.reshape(e, k, n) * global_scale[0]
        key = jax.random.key(seed)
        ks = jax.random.split(key, 6)
        hidden_states = jax.random.normal(ks[0], (B, S, H), dtype=jnp.float32)
        gate_weight = jax.random.normal(ks[1], (E, H), dtype=jnp.float32) * 0.02
        fc_up_qweights = jax.random.randint(ks[2], (E, H, I), 0, 16, dtype=jnp.int32)
        fc_up_blocks_scale = jax.random.uniform(ks[3], (E, H // GROUP, I), dtype=jnp.float32) * 0.02
        fc_up_global_scale = jnp.ones((1,), dtype=jnp.float32)
        fc_down_qweights = jax.random.randint(ks[4], (E, I, H), 0, 16, dtype=jnp.int32)
        fc_down_blocks_scale = jax.random.uniform(ks[5], (E, I // GROUP, H), dtype=jnp.float32) * 0.02
        fc_down_global_scale = jnp.ones((1,), dtype=jnp.float32)
        return {'hidden_states': hidden_states, 'gate_weight': gate_weight, 'fc_up_blocks_scale': fc_up_blocks_scale, 'fc_up_global_scale': fc_up_global_scale, 'fc_down_blocks_scale': fc_down_blocks_scale, 'fc_down_global_scale': fc_down_global_scale, 'fc_up_qweights': fc_up_qweights, 'fc_down_qweights': fc_down_qweights}
    _L3_ffn_all = _L3_ffn_setup()
    _L3_ffn_in = {k: v for k, v in _L3_ffn_all.items() if k in ('gate_weight', 'fc_up_blocks_scale', 'fc_up_global_scale', 'fc_down_blocks_scale', 'fc_down_global_scale', 'fc_up_qweights', 'fc_down_qweights')}
    del _L3_ffn_all
    return {'x': x, 'fside_BxSxS_0': fside_BxSxS_0, 'cond_512': cond_512, 'L0_cond_w': _L0_cond_in['w'], 'L0_cond_u': _L0_cond_in['u'], 'L0_ffn_gate_weight': _L0_ffn_in['gate_weight'], 'L0_ffn_gate_up_proj': _L0_ffn_in['gate_up_proj'], 'L0_ffn_down_proj': _L0_ffn_in['down_proj'], 'L0_ffn_old_to_new': _L0_ffn_in['old_to_new'], 'L1_cond_w': _L1_cond_in['w'], 'L1_cond_u': _L1_cond_in['u'], 'L1_ffn_router_w': _L1_ffn_in['router_w'], 'L1_ffn_wg': _L1_ffn_in['wg'], 'L1_ffn_wu': _L1_ffn_in['wu'], 'L1_ffn_wd': _L1_ffn_in['wd'], 'L1_ffn_sg': _L1_ffn_in['sg'], 'L1_ffn_su': _L1_ffn_in['su'], 'L1_ffn_sd': _L1_ffn_in['sd'], 'L2_cond_w': _L2_cond_in['w'], 'L2_cond_u': _L2_cond_in['u'], 'L2_ffn_gate_w': _L2_ffn_in['gate_w'], 'L2_ffn_cls_w': _L2_ffn_in['cls_w'], 'L2_ffn_extra_scale': _L2_ffn_in['extra_scale'], 'L2_ffn_extra_bias': _L2_ffn_in['extra_bias'], 'L2_ffn_wg': _L2_ffn_in['wg'], 'L2_ffn_wu': _L2_ffn_in['wu'], 'L2_ffn_wd': _L2_ffn_in['wd'], 'L2_ffn_sg': _L2_ffn_in['sg'], 'L2_ffn_su': _L2_ffn_in['su'], 'L2_ffn_sd': _L2_ffn_in['sd'], 'L3_cond_w': _L3_cond_in['w'], 'L3_cond_u': _L3_cond_in['u'], 'L3_ffn_gate_weight': _L3_ffn_in['gate_weight'], 'L3_ffn_fc_up_blocks_scale': _L3_ffn_in['fc_up_blocks_scale'], 'L3_ffn_fc_up_global_scale': _L3_ffn_in['fc_up_global_scale'], 'L3_ffn_fc_down_blocks_scale': _L3_ffn_in['fc_down_blocks_scale'], 'L3_ffn_fc_down_global_scale': _L3_ffn_in['fc_down_global_scale'], 'L3_ffn_fc_up_qweights': _L3_ffn_in['fc_up_qweights'], 'L3_ffn_fc_down_qweights': _L3_ffn_in['fc_down_qweights']}

def reference(x, fside_BxSxS_0, cond_512, L0_cond_w, L0_cond_u, L0_ffn_gate_weight, L0_ffn_gate_up_proj, L0_ffn_down_proj, L0_ffn_old_to_new, L1_cond_w, L1_cond_u, L1_ffn_router_w, L1_ffn_wg, L1_ffn_wu, L1_ffn_wd, L1_ffn_sg, L1_ffn_su, L1_ffn_sd, L2_cond_w, L2_cond_u, L2_ffn_gate_w, L2_ffn_cls_w, L2_ffn_extra_scale, L2_ffn_extra_bias, L2_ffn_wg, L2_ffn_wu, L2_ffn_wd, L2_ffn_sg, L2_ffn_su, L2_ffn_sd, L3_cond_w, L3_cond_u, L3_ffn_gate_weight, L3_ffn_fc_up_blocks_scale, L3_ffn_fc_up_global_scale, L3_ffn_fc_down_blocks_scale, L3_ffn_fc_down_global_scale, L3_ffn_fc_up_qweights, L3_ffn_fc_down_qweights):
    import jax
    import jax.numpy as jnp

    def _L0_cond_ref(r, k, v, w, u, time_emb):
        import jax, jax.numpy as jnp
        from jax import lax
        import numpy as np
        B, T, C, TD = (8, 256, 256, 64)

        def _bi_wkv(r, k, v, w, u, time_emb):
            tf = jax.nn.sigmoid(jnp.sum(time_emb, axis=-1))[:, None, None]
            decay = jnp.exp(-jnp.exp(w.astype(jnp.float32)))[None, :] * (0.5 + 0.5 * tf[:, :, 0])
            kf = k.astype(jnp.float32)
            vf = v.astype(jnp.float32)
            ek = jnp.exp(jnp.minimum(kf, 30.0))
            ekv = ek * vf

            def step(carry, x):
                a, b = carry
                ekv_t, ek_t = x
                a = a * decay + ekv_t
                b = b * decay + ek_t
                return ((a, b), (a, b))
            ekv_t = jnp.swapaxes(ekv, 0, 1)
            ek_t = jnp.swapaxes(ek, 0, 1)
            init = (jnp.zeros_like(decay), jnp.zeros_like(decay))
            _, (nf, df) = lax.scan(step, init, (ekv_t, ek_t))
            _, (nb, db) = lax.scan(step, init, (ekv_t, ek_t), reverse=True)
            nf = jnp.swapaxes(nf, 0, 1)
            df = jnp.swapaxes(df, 0, 1)
            nb = jnp.swapaxes(nb, 0, 1)
            db = jnp.swapaxes(db, 0, 1)
            euk = jnp.exp(jnp.minimum(u.astype(jnp.float32)[None, None, :] + kf, 30.0))
            num = nf + nb - ekv + euk * vf
            den = df + db - ek + euk
            base = jax.nn.sigmoid(r.astype(jnp.float32)) * (num / jnp.maximum(den, 1e-08))
            out = base * (0.8 + 0.2 * tf)
            return out.astype(r.dtype)
        return _bi_wkv(r, k, v, w, u, time_emb)

    def _L0_ffn_ref(hidden_states, gate_weight, gate_up_proj, down_proj, old_to_new):
        import jax, jax.numpy as jnp
        import numpy as np
        NUM_EXPERTS = 128
        NUM_KEPT = 48
        TOP_K = 8
        HIDDEN = 256
        INTER = 96
        CAP = 96
        BATCH, SEQ = (2, 128)
        B, S, H = hidden_states.shape
        x = hidden_states.reshape(-1, H)
        T = x.shape[0]
        logits = x @ gate_weight.T
        logits = jnp.where(old_to_new[None, :] == -1, -jnp.inf, logits)
        probs = jax.nn.softmax(logits.astype(jnp.float32), axis=-1).astype(logits.dtype)
        top_v, top_i = jax.lax.top_k(probs, TOP_K)
        top_v = top_v / jnp.sum(top_v, axis=-1, keepdims=True)
        sel_new = old_to_new[top_i]
        E = gate_up_proj.shape[0]
        flat_e = sel_new.reshape(-1)
        flat_w = top_v.reshape(-1)
        tok = jnp.repeat(jnp.arange(T), TOP_K)
        oh = (flat_e[:, None] == jnp.arange(E)[None, :]).astype(jnp.int32)
        pos = jnp.sum(jnp.cumsum(oh, axis=0) * oh, axis=-1) - 1
        valid = pos < CAP
        pos_c = jnp.where(valid, pos, CAP)
        xb = jnp.zeros((E, CAP + 1, H), x.dtype).at[flat_e, pos_c].set(x[tok])
        xb = xb[:, :CAP]
        gu = jnp.einsum('ech,eoh->eco', xb, gate_up_proj)
        g, u = jnp.split(gu, 2, axis=-1)
        h = jax.nn.silu(g) * u
        out = jnp.einsum('eci,ehi->ech', h, down_proj)
        y = out[flat_e, jnp.minimum(pos_c, CAP - 1)]
        w = flat_w * valid.astype(flat_w.dtype)
        final = jnp.zeros_like(x).at[tok].add(y * w[:, None])
        return final.reshape(B, S, H)

    def _L1_cond_ref(r, k, v, w, u, time_emb):
        import jax, jax.numpy as jnp
        from jax import lax
        import numpy as np
        B, T, C, TD = (8, 256, 256, 64)

        def _bi_wkv(r, k, v, w, u, time_emb):
            tf = jax.nn.sigmoid(jnp.sum(time_emb, axis=-1))[:, None, None]
            decay = jnp.exp(-jnp.exp(w.astype(jnp.float32)))[None, :] * (0.5 + 0.5 * tf[:, :, 0])
            kf = k.astype(jnp.float32)
            vf = v.astype(jnp.float32)
            ek = jnp.exp(jnp.minimum(kf, 30.0))
            ekv = ek * vf

            def step(carry, x):
                a, b = carry
                ekv_t, ek_t = x
                a = a * decay + ekv_t
                b = b * decay + ek_t
                return ((a, b), (a, b))
            ekv_t = jnp.swapaxes(ekv, 0, 1)
            ek_t = jnp.swapaxes(ek, 0, 1)
            init = (jnp.zeros_like(decay), jnp.zeros_like(decay))
            _, (nf, df) = lax.scan(step, init, (ekv_t, ek_t))
            _, (nb, db) = lax.scan(step, init, (ekv_t, ek_t), reverse=True)
            nf = jnp.swapaxes(nf, 0, 1)
            df = jnp.swapaxes(df, 0, 1)
            nb = jnp.swapaxes(nb, 0, 1)
            db = jnp.swapaxes(db, 0, 1)
            euk = jnp.exp(jnp.minimum(u.astype(jnp.float32)[None, None, :] + kf, 30.0))
            num = nf + nb - ekv + euk * vf
            den = df + db - ek + euk
            base = jax.nn.sigmoid(r.astype(jnp.float32)) * (num / jnp.maximum(den, 1e-08))
            out = base * (0.8 + 0.2 * tf)
            return out.astype(r.dtype)
        return _bi_wkv(r, k, v, w, u, time_emb)

    def _L1_ffn_ref(x, router_w, wg, wu, wd, sg, su, sd):
        import jax, jax.numpy as jnp
        import numpy as np
        from jax import lax
        E = 8
        K = 2
        D = 256
        H = 176
        NS = 2
        B, T = (2, 256)
        EPS = 1e-20
        HS = H * NS

        def _silu(v):
            return v * jax.nn.sigmoid(v)
        b, t, d = x.shape
        xf = x.reshape(b * t, d)
        n = xf.shape[0]
        gates = jax.nn.softmax(xf @ router_w.T, axis=-1)
        topv, topi = lax.top_k(gates, K)
        masked = jnp.zeros_like(gates).at[jnp.arange(n)[:, None], topi].set(topv)
        masked = masked / (masked.sum(axis=-1, keepdims=True) + EPS)

        def step(acc, p):
            wg_e, wu_e, wd_e, g_e = p
            y = _silu(xf @ wg_e) * (xf @ wu_e) @ wd_e
            return (acc + y * g_e[:, None], None)
        routed, _ = lax.scan(step, jnp.zeros_like(xf), (wg, wu, wd, masked.T))
        shared = _silu(xf @ sg) * (xf @ su) @ sd
        return (routed + shared).reshape(b, t, d)

    def _L2_cond_ref(r, k, v, w, u, time_emb):
        import jax, jax.numpy as jnp
        from jax import lax
        import numpy as np
        B, T, C, TD = (8, 256, 256, 64)

        def _bi_wkv(r, k, v, w, u, time_emb):
            tf = jax.nn.sigmoid(jnp.sum(time_emb, axis=-1))[:, None, None]
            decay = jnp.exp(-jnp.exp(w.astype(jnp.float32)))[None, :] * (0.5 + 0.5 * tf[:, :, 0])
            kf = k.astype(jnp.float32)
            vf = v.astype(jnp.float32)
            ek = jnp.exp(jnp.minimum(kf, 30.0))
            ekv = ek * vf

            def step(carry, x):
                a, b = carry
                ekv_t, ek_t = x
                a = a * decay + ekv_t
                b = b * decay + ek_t
                return ((a, b), (a, b))
            ekv_t = jnp.swapaxes(ekv, 0, 1)
            ek_t = jnp.swapaxes(ek, 0, 1)
            init = (jnp.zeros_like(decay), jnp.zeros_like(decay))
            _, (nf, df) = lax.scan(step, init, (ekv_t, ek_t))
            _, (nb, db) = lax.scan(step, init, (ekv_t, ek_t), reverse=True)
            nf = jnp.swapaxes(nf, 0, 1)
            df = jnp.swapaxes(df, 0, 1)
            nb = jnp.swapaxes(nb, 0, 1)
            db = jnp.swapaxes(db, 0, 1)
            euk = jnp.exp(jnp.minimum(u.astype(jnp.float32)[None, None, :] + kf, 30.0))
            num = nf + nb - ekv + euk * vf
            den = df + db - ek + euk
            base = jax.nn.sigmoid(r.astype(jnp.float32)) * (num / jnp.maximum(den, 1e-08))
            out = base * (0.8 + 0.2 * tf)
            return out.astype(r.dtype)
        return _bi_wkv(r, k, v, w, u, time_emb)

    def _L2_ffn_ref(x, gate_w, cls_w, extra_scale, extra_bias, wg, wu, wd, sg, su, sd):
        import jax, jax.numpy as jnp
        import numpy as np
        TOPK = 2
        HID, INTER, E, SHARED_INTER = (256, 176, 14, 352)
        shape = x.shape
        d = shape[-1]
        xf = x.reshape(-1, d)
        T = xf.shape[0]
        n_exp = gate_w.shape[0]
        logits = xf @ cls_w.T * jax.nn.silu(xf @ gate_w.T)
        scores = jax.nn.softmax(jnp.abs(logits).astype(jnp.float32), axis=-1)
        biased = scores + extra_bias[None, :]
        _, idx = jax.lax.top_k(biased, TOPK)
        orig = 1.0 + scores * extra_scale[None, :]
        w = jnp.take_along_axis(orig, idx, axis=1).astype(x.dtype)
        combine = jnp.zeros((T, n_exp), x.dtype).at[jnp.arange(T)[:, None], idx].add(w)
        g = jax.nn.silu(jnp.einsum('td,efd->etf', xf, wg))
        u = jnp.einsum('td,efd->etf', xf, wu)
        o = jnp.einsum('etf,edf->etd', g * u, wd)
        y = jnp.einsum('etd,te->td', o, combine)
        z = jax.nn.silu(xf @ sg.T) * (xf @ su.T) @ sd.T
        return (y + z).reshape(shape)

    def _L3_cond_ref(r, k, v, w, u, time_emb):
        import jax, jax.numpy as jnp
        from jax import lax
        import numpy as np
        B, T, C, TD = (8, 256, 256, 64)

        def _bi_wkv(r, k, v, w, u, time_emb):
            tf = jax.nn.sigmoid(jnp.sum(time_emb, axis=-1))[:, None, None]
            decay = jnp.exp(-jnp.exp(w.astype(jnp.float32)))[None, :] * (0.5 + 0.5 * tf[:, :, 0])
            kf = k.astype(jnp.float32)
            vf = v.astype(jnp.float32)
            ek = jnp.exp(jnp.minimum(kf, 30.0))
            ekv = ek * vf

            def step(carry, x):
                a, b = carry
                ekv_t, ek_t = x
                a = a * decay + ekv_t
                b = b * decay + ek_t
                return ((a, b), (a, b))
            ekv_t = jnp.swapaxes(ekv, 0, 1)
            ek_t = jnp.swapaxes(ek, 0, 1)
            init = (jnp.zeros_like(decay), jnp.zeros_like(decay))
            _, (nf, df) = lax.scan(step, init, (ekv_t, ek_t))
            _, (nb, db) = lax.scan(step, init, (ekv_t, ek_t), reverse=True)
            nf = jnp.swapaxes(nf, 0, 1)
            df = jnp.swapaxes(df, 0, 1)
            nb = jnp.swapaxes(nb, 0, 1)
            db = jnp.swapaxes(db, 0, 1)
            euk = jnp.exp(jnp.minimum(u.astype(jnp.float32)[None, None, :] + kf, 30.0))
            num = nf + nb - ekv + euk * vf
            den = df + db - ek + euk
            base = jax.nn.sigmoid(r.astype(jnp.float32)) * (num / jnp.maximum(den, 1e-08))
            out = base * (0.8 + 0.2 * tf)
            return out.astype(r.dtype)
        return _bi_wkv(r, k, v, w, u, time_emb)

    def _L3_ffn_ref(hidden_states, gate_weight, fc_up_blocks_scale, fc_up_global_scale, fc_down_blocks_scale, fc_down_global_scale, fc_up_qweights, fc_down_qweights):
        import jax, jax.numpy as jnp
        import numpy as np
        E, TOP_K, H, I = (16, 2, 256, 128)
        B, S = (2, 256)
        GROUP = 16
        RSF = 1.0

        def _dequant(q, blocks_scale, global_scale):
            e, k, n = q.shape
            w = (q.astype(jnp.float32) - 8.0).reshape(e, k // GROUP, GROUP, n)
            w = w * blocks_scale[:, :, None, :]
            return w.reshape(e, k, n) * global_scale[0]
        b, s, h = hidden_states.shape
        x = hidden_states.reshape(-1, h).astype(jnp.float32)
        t = x.shape[0]
        logits = jax.nn.log_sigmoid(x @ gate_weight.T)
        probs = jax.nn.softmax(logits, axis=-1)
        topw, topi = jax.lax.top_k(probs, TOP_K)
        topw = topw / (jnp.sum(topw, axis=-1, keepdims=True) + 1e-20)
        wdense = jnp.zeros((t, E), dtype=jnp.float32)
        wdense = wdense.at[jnp.arange(t)[:, None], topi].add(topw) * RSF
        w_up = _dequant(fc_up_qweights, fc_up_blocks_scale, fc_up_global_scale)
        w_down = _dequant(fc_down_qweights, fc_down_blocks_scale, fc_down_global_scale)
        z = jnp.einsum('th,ehi->tei', x, w_up)
        a = jnp.square(jnp.maximum(z, 0.0))
        aw = a * wdense[:, :, None]
        y = jnp.einsum('tei,eih->th', aw, w_down)
        return y.reshape(b, s, h)
    x = x + _L0_ffn_ref(_L0_cond_ref(x, fside_BxSxS_0, fside_BxSxS_0, L0_cond_w, L0_cond_u, cond_512), L0_ffn_gate_weight, L0_ffn_gate_up_proj, L0_ffn_down_proj, L0_ffn_old_to_new)
    x = x + _L1_ffn_ref(_L1_cond_ref(x, fside_BxSxS_0, fside_BxSxS_0, L1_cond_w, L1_cond_u, cond_512), L1_ffn_router_w, L1_ffn_wg, L1_ffn_wu, L1_ffn_wd, L1_ffn_sg, L1_ffn_su, L1_ffn_sd)
    x = x + _L2_ffn_ref(_L2_cond_ref(x, fside_BxSxS_0, fside_BxSxS_0, L2_cond_w, L2_cond_u, cond_512), L2_ffn_gate_w, L2_ffn_cls_w, L2_ffn_extra_scale, L2_ffn_extra_bias, L2_ffn_wg, L2_ffn_wu, L2_ffn_wd, L2_ffn_sg, L2_ffn_su, L2_ffn_sd)
    x = x + _L3_ffn_ref(_L3_cond_ref(x, fside_BxSxS_0, fside_BxSxS_0, L3_cond_w, L3_cond_u, cond_512), L3_ffn_gate_weight, L3_ffn_fc_up_blocks_scale, L3_ffn_fc_up_global_scale, L3_ffn_fc_down_blocks_scale, L3_ffn_fc_down_global_scale, L3_ffn_fc_up_qweights, L3_ffn_fc_down_qweights)
    return x

_drawn_inputs = setup_inputs


def setup_inputs(seed=0):
    import zlib

    import numpy as np

    out = dict(_drawn_inputs(seed))
    spreads = {}
    factors = {'cond_512': 8.0,
     'L0_cond_w': 8.0,
     'L0_cond_u': 8.0,
     'L0_ffn_gate_weight': 8.0,
     'L0_ffn_gate_up_proj': 8.0,
     'L0_ffn_down_proj': 8.0,
     'L1_cond_w': 8.0,
     'L1_cond_u': 8.0,
     'L1_ffn_router_w': 8.0,
     'L1_ffn_wg': 8.0,
     'L1_ffn_wu': 8.0,
     'L1_ffn_wd': 8.0,
     'L1_ffn_sg': 8.0,
     'L1_ffn_su': 8.0,
     'L1_ffn_sd': 8.0,
     'L2_cond_w': 8.0,
     'L2_cond_u': 8.0,
     'L2_ffn_gate_w': 8.0,
     'L2_ffn_cls_w': 8.0,
     'L2_ffn_extra_scale': 8.0,
     'L2_ffn_extra_bias': 8.0,
     'L2_ffn_wg': 8.0,
     'L2_ffn_wu': 8.0,
     'L2_ffn_wd': 8.0,
     'L2_ffn_sg': 8.0,
     'L2_ffn_su': 8.0,
     'L2_ffn_sd': 8.0,
     'L3_cond_u': 4.28,
     'L3_ffn_fc_up_blocks_scale': 2.764,
     'L3_ffn_fc_down_blocks_scale': 3.621}
    for name, (base, spread) in spreads.items():
        noise = np.random.default_rng([zlib.crc32(name.encode()), seed]).standard_normal(out[name].shape)
        drawn = base * np.exp(spread * noise) if base else spread * noise
        out[name] = jnp.asarray(drawn.astype(out[name].dtype))
    for name, factor in factors.items():
        out[name] = (out[name] * factor).astype(out[name].dtype)
    return out
```

```python
from contextlib import ExitStack

import concourse.bass as bass
from concourse import mybir

P = 128
NB, NT, C = 4, 256, 256
TOK = NB * NT
KT = C // P
HALF = TOK // 2
TT = TOK // P
NL = 4
TD = 64
UNITS = KT * NB

E0, KEPT, TOP0, CAP, I0 = 128, 48, 8, 96, 96
E1, I1, SH1 = 8, 176, 352
E2, I2, SH2 = 14, 176, 352
E3, I3, GROUP = 16, 128, 16
EPS = 1e-20

CH = [KEPT * I0 // P, -(-(E1 * I1 + SH1) // P), (E2 * I2 + SH2) // P, E3]
C0 = [sum(CH[:l]) for l in range(NL)]
S0 = [2 * c for c in C0]
GLU = C0[3]
KG = [2 * KEPT, 2 * (E1 + 1), 2 * (E2 + 1), 2 * E3]
WC = 3 * KT * P
GW = [E0, E1, 2 * E2, E3]
G0 = [sum(GW[:l]) for l in range(NL)]
NG = P // GROUP
QLOADS = 2 + KT + 1
assert all(c % 2 == 0 for c in CH)

F32, F32R, BF16, I32, U32 = (mybir.dt.float32, mybir.dt.float32r, mybir.dt.bfloat16,
                             mybir.dt.int32, mybir.dt.uint32)
ALU = mybir.AluOpType
ACT = mybir.ActivationFunctionType
AX = mybir.AxisListType.X


def wait(eng, sem, value):
    if not isinstance(value, int) or value > 0:
        eng.wait_ge(sem, value)


def steps(eng, layer, body, inner=None, n_inner=0):
    s0, c0, n = S0[layer], C0[layer], 2 * CH[layer]
    for k in range(3):
        body(s0 + k, c0 + k // 2, k)
    trips = (n - 4) // 4
    if inner is not None:
        with eng.Fori(0, n_inner) as i:
            inner(i, lambda: [body(i * 4 + (s0 + k), i * 2 + (c0 + k // 2), k) for k in range(3, 5)],
                  lambda: [body(i * 4 + (s0 + k), i * 2 + (c0 + k // 2), k) for k in range(5, 7)])
    if n_inner < trips:
        with eng.Fori(n_inner, trips) as i:
            for k in range(3, 7):
                body(i * 4 + (s0 + k), i * 2 + (c0 + k // 2), k)
    body(s0 + n - 1, c0 + CH[layer] - 1, n - 1)


def build(nc, xT, fT, cond, wu, o2n_row, o2n_col, gwT, rconst, gscale, wglu, wq, s_up, s_down, sel3,
          ident, tri, iota, out):
    with ExitStack() as ctx:
        def sb(name, shape, dt=F32):
            return ctx.enter_context(nc.sbuf_tensor(name, shape, dt))

        def sem(name):
            return ctx.enter_context(nc.semaphore(name))

        x = sb("x", [P, KT, TOK])
        cnd = sb("cnd", [P, KT, TOK])
        c_hi = sb("c_hi", [P, KT, TOK], F32R)
        c_lo = sb("c_lo", [P, KT, TOK], F32R)
        R = sb("R", [P, NL * UNITS, NT])
        fs = sb("fs", [P, UNITS, NT])
        ek = sb("ek", [P, UNITS, NT])
        ekv = sb("ekv", [P, UNITS, NT])
        ek_rev = sb("ek_rev", [P, UNITS, NT])
        ekv_rev = sb("ekv_rev", [P, UNITS, NT])
        fwd = sb("fwd", [P, 2, 2, NT])
        bwd = sb("bwd", [P, 2, 2, NT])
        dif = sb("dif", [P, 2, 2, NT])
        te = sb("te", [P, NB, TD])
        tfs = sb("tfs", [P, NB])
        tf = sb("tf", [P, NB])
        tdec = sb("tdec", [P, NB])
        wus = sb("wus", [P, NL, 2, KT])
        wexp = sb("wexp", [P, NL, KT])
        decay = sb("decay", [P, NL * UNITS])
        oscale = sb("oscale", [P, NL * UNITS])
        raw = sb("raw", [P, 2, WC + P])
        raw_q = sb("raw_q", [P, 2, 2 * C], I32)
        raw_s = sb("raw_s", [P, 2, 2 * C])
        raw_sel = sb("raw_sel", [KG[3], 2, P])
        w_hi = sb("w_hi", [P, 2, WC + P], F32R)
        w_lo = sb("w_lo", [P, 2, WC], F32R)
        act_g = sb("act_g", [P, 2, HALF])
        t = sb("t", [P, 2, HALF])
        h = sb("h", [P, 2, HALF])
        h_hi = sb("h_hi", [P, 2, HALF], F32R)
        h_lo = sb("h_lo", [P, 2, HALF], F32R)
        gws = sb("gws", [P, KT, sum(GW)])
        gates = sb("gates", [P, TOK], F32R)
        lg = sb("lg", [P, TT, E0])
        ex = sb("ex", [P, TT, E0])
        sel = sb("sel", [P, TT, E0])
        sel16 = sb("sel16", [P, TT, E0], BF16)
        gcat = sb("gcat", [P, TT, E0], F32R)
        gold = sb("gold", [P, 2, TOK], F32R)
        v8 = sb("v8", [P, TT, 8])
        i8 = sb("i8", [P, TT, 8], U32)
        if8 = sb("if8", [P, TT, 2])
        r8 = sb("r8", [P, 4, TT])
        rcs = sb("rcs", [P, 2, E2])
        gsc = sb("gsc", [P, 2])
        keep_i = sb("keep_i", [P, E0], I32)
        keep = sb("keep", [P, 2, E0])
        o2n_ci = sb("o2n_ci", [P, 1], I32)
        o2n_c = sb("o2n_c", [P, 1])
        remap = sb("remap", [P, 2, 2 * KEPT], F32R)
        ident_s = sb("ident_s", [P, P])
        tri_s = sb("tri_s", [P, P])
        tri16 = sb("tri16", [P, P], BF16)
        ones16 = sb("ones16", [P, P], BF16)
        iota_s = sb("iota_s", [P, E0])

        y_ps = ctx.enter_context(nc.psum_tensor("y_ps", [P, KT, 2, HALF], F32))
        g_ps = ctx.enter_context(nc.psum_tensor("g_ps", [P, 2, HALF], F32))
        u_ps = ctx.enter_context(nc.psum_tensor("u_ps", [P, HALF], F32))
        r_ps = ctx.enter_context(nc.psum_tensor("r_ps", [P, 512], F32))

        in_x, in_fs, in_te, in_wu = sem("in_x"), sem("in_fs"), sem("in_te"), sem("in_wu")
        in_gw, in_rc = sem("in_gw"), sem("in_rc")
        raw_in = [sem("raw_in0"), sem("raw_in1")]
        q_in = [sem("q_in0"), sem("q_in1")]
        w_hi_ready, w_lo_ready, w_deq = sem("w_hi_ready"), sem("w_lo_ready"), sem("w_deq")
        w_deq_part, sum_ready = sem("w_deq_part"), sem("sum_ready")
        g_ready, u_ready, gate_ready = sem("g_ready"), sem("u_ready"), sem("gate_ready")
        act_ready, t_ready, h_ready = sem("act_ready"), sem("t_ready"), sem("h_ready")
        h_hi_ready, h_lo_ready, y_done = sem("h_hi_ready"), sem("h_lo_ready"), sem("y_done")
        x_ready, sig_ready, c_ready = sem("x_ready"), sem("sig_ready"), sem("c_ready")
        c_hi_ready, c_lo_ready = sem("c_hi_ready"), sem("c_lo_ready")
        logits_ready, lgt, rexp, rpe, gcat_ready = (sem("logits_ready"), sem("lgt"), sem("rexp"),
                                                    sem("rpe"), sem("gcat_ready"))
        turned, gates_ready = sem("turned"), sem("gates_ready")
        dve_done, act_done = sem("dve_done"), sem("act_done")
        tf_ready, kexp_ready, ekv_ready = sem("tf_ready"), sem("kexp_ready"), sem("ekv_ready")
        uk_ready, euk_ready, wexp_ready = sem("uk_ready"), sem("euk_ready"), sem("wexp_ready")
        dif_ready, scan_ready, num_ready, R_ready = (sem("dif_ready"), sem("scan_ready"),
                                                     sem("num_ready"), sem("R_ready"))
        out_done = sem("out_done")

        block = ctx.enter_context(nc.Block())

        BLOCKS = [(hf, m) for hf in range(2) for m in range(KT)]

        def blk(tensor, hf, m):
            return tensor[:, m, hf * HALF:(hf + 1) * HALF]

        def unit(tensor, q):
            return tensor[:, bass.ds(q, 1), :].rearrange("p a n -> p (a n)")

        @block.sync
        def _(sp):
            def load_glu(c, slot):
                wait(sp, w_lo_ready, c - 1)
                sp.dma_start(raw[:, slot, :], wglu[bass.ds(c, 1)].rearrange("a p n -> p (a n)")
                             ).then_inc(raw_in[slot], 16)

            sp.dma_start(fs[:, :, :].rearrange("p (k b) n -> p k (b n)", k=KT),
                         fT.rearrange("k p n -> p k n")).then_inc(in_fs, 16)
            sp.dma_start(te[:, :, :].rearrange("p b n -> p (b n)"), cond.to_broadcast([P, NB * TD])
                         ).then_inc(in_te, 16)
            sp.dma_start(wus[:, :, :, :].rearrange("p a b c -> p (a b c)"), wu).then_inc(in_wu, 16)
            sp.dma_start(x[:, :, :], xT.rearrange("k p n -> p k n")).then_inc(in_x, 16)
            for dst, src in ((keep_i[:, :], o2n_row.to_broadcast([P, E0])), (o2n_ci[:, :], o2n_col),
                             (rcs[:, :, :].rearrange("p a n -> p (a n)"),
                              rconst.to_broadcast([P, 2 * E2])),
                             (gsc[:, :], gscale.to_broadcast([P, 2])),
                             (ident_s[:, :], ident), (tri_s[:, :], tri), (iota_s[:, :], iota)):
                sp.dma_start(dst, src).then_inc(in_rc, 16)
            sp.dma_start(gws[:, :, :], gwT).then_inc(in_gw, 16)
            load_glu(0, 0)
            load_glu(1, 1)
            with sp.Fori(1, GLU // 2) as i:
                load_glu(i * 2, 0)
                load_glu(i * 2 + 1, 1)

            def load_q(e, slot):
                ex_ = slice(e, e + 1) if isinstance(e, int) else bass.ds(e, 1)
                sp.dma_start(raw_q[:, slot, :], wq[ex_].rearrange("a p n -> p (a n)")
                             ).then_inc(q_in[slot], 16)
                for k in range(KT + 1):
                    src = s_up[ex_, k * NG:(k + 1) * NG, :] if k < KT else s_down[ex_]
                    cols = slice(k * P, (k + 1) * P) if k < KT else slice(C, 2 * C)
                    n = src.shape[2]
                    src = src.rearrange("a g n -> (a g) n").unsqueeze(1).to_broadcast([NG, GROUP, n])
                    sp.dma_start(raw_s[:, slot, cols], src
                                 ).then_inc(q_in[slot], 16)
                sp.dma_start(raw_sel[:, slot, :], sel3[ex_].rearrange("a p n -> p (a n)")
                             ).then_inc(q_in[slot], 16)

            load_q(0, 0)
            load_q(1, 1)
            with sp.Fori(1, E3 // 2) as i:
                for slot in range(2):
                    sp.wait_ge(w_lo_ready, i * 2 + (GLU + slot - 1))
                    load_q(i * 2 + slot, slot)
            for n, (hf, m) in enumerate(BLOCKS):
                sp.wait_ge(x_ready, (NL - 1) * len(BLOCKS) + n + 1)
                sp.dma_start(out[m, :, hf * HALF:(hf + 1) * HALF], blk(x, hf, m)).then_inc(out_done, 16)
            sp.wait_ge(out_done, 16 * len(BLOCKS))

        @block.tensor
        def _(pe):
            def split_mm(dst, w_at, rhs_hi, rhs_lo, start, stop):
                n = 0
                for slot, cols, k in w_at:
                    for w, r in ((w_hi, rhs_hi), (w_hi, rhs_lo), (w_lo, rhs_hi)):
                        n += 1
                        mm = pe.matmul(dst, w[:, slot, cols], r(k), start=start and n == 1,
                                       stop=stop and n == 3 * len(w_at), skip_group_check=True)
                return mm

            def up(layer, gs, c, k):
                hf, par, slot = k % 2, k % 2, (k // 2) % 2
                tok = slice(hf * HALF, (hf + 1) * HALF)

                def col(j):
                    return slice(j * P, (j + 1) * P)

                def hi(kt):
                    return c_hi[:, kt, tok]

                def lo(kt):
                    return c_lo[:, kt, tok]

                if hf == 0:
                    pe.wait_ge(w_lo_ready, c + 1)
                if k < 2:
                    pe.wait_ge(c_lo_ready, 4 * layer + 2 * hf + 2)
                wait(pe, h_ready, gs - 1)
                split_mm(g_ps[:, par, :], [(slot, col(j), j) for j in range(KT)], hi, lo,
                         True, True).then_inc(g_ready, 1)
                if layer < 3:
                    wait(pe, t_ready, gs)
                    split_mm(u_ps[:, :], [(slot, col(KT + j), j) for j in range(KT)], hi, lo,
                             True, True).then_inc(u_ready, 1)

            def gate(layer, gs, c, k):
                hf, par, slot = k % 2, k % 2, (k // 2) % 2
                tok = slice(hf * HALF, (hf + 1) * HALF)
                if k < 1:
                    pe.wait_ge(gates_ready, 2 * layer + 2)
                wait(pe, act_ready, gs + 1)
                if layer == 3:
                    wait(pe, h_ready, gs)
                pe.matmul(g_ps[:, par, :] if layer < 3 else u_ps[:, :],
                          w_hi[0:KG[layer], slot, WC:WC + P], gates[0:KG[layer], tok],
                          start=True, stop=True, skip_group_check=True).then_inc(gate_ready, 1)

            def down(layer, gs, k, start):
                first = KT if layer == 3 else 2 * KT
                hf, par, slot = k % 2, k % 2, (k // 2) % 2
                pe.wait_ge(h_lo_ready, gs + 1)
                for m in range(KT):
                    mm = split_mm(y_ps[:, m, hf, :],
                                  [(slot, slice((first + m) * P, (first + m + 1) * P), 0)],
                                  lambda _: h_hi[:, par, :], lambda _: h_lo[:, par, :], start, False)
                mm.then_inc(y_done, 1)

            def logits(layer, dst, tiles, n0):
                for i in tiles:
                    for kt in range(KT):
                        mm = pe.matmul(dst(i), cnd[:, kt, i * P:(i + 1) * P],
                                       gws[:, kt, G0[layer]:G0[layer] + GW[layer]],
                                       start=kt == 0, stop=kt == KT - 1, skip_group_check=True)
                return mm

            def router(layer):
                pe.wait_ge(c_ready, 4 * layer + 4)
                if layer == 0:
                    pe.wait_ge(in_gw, 16)
                n = GW[layer]
                if layer:
                    logits(layer, lambda i: r_ps[:, i * n:(i + 1) * n], range(TT), 0
                           ).then_inc(logits_ready, 1)
                else:
                    yf = y_ps[:, 0, :, :].rearrange("p a n -> p (a n)")
                    logits(0, lambda i: yf[:, i * n:(i + 1) * n], range(TT), 0).then_inc(logits_ready, 1)

            def positions():
                pos = y_ps[:, 1, :, :].rearrange("p a n -> p (a n)")
                pe.wait_ge(rpe, 1)
                for i in range(TT):
                    for j in range(i + 1):
                        mm = pe.matmul(pos[:, i * E0:(i + 1) * E0],
                                       (tri16 if j == i else ones16)[:, :], sel16[:, j, :],
                                       start=j == 0, stop=j == i, skip_group_check=True)
                mm.then_inc(logits_ready, 1)

            def turn(layer):
                if layer == 0:
                    yf = y_ps[:, :, :, :].rearrange("p a b n -> p (a b n)")
                    pe.wait_ge(gcat_ready, 1)
                    gh = [gcat[:, :, :].bitcast(F32), lg[:, :, :]]
                    for part in range(2):
                        for i in range(TT):
                            mm = pe.transpose(yf[:, part * TOK + i * P:part * TOK + (i + 1) * P],
                                              gh[part][:, i, :], ident_s[:, :])
                    mm.then_inc(turned, 1)
                    pe.wait_ge(rexp, 5)
                    for hf in range(2):
                        if hf:
                            pe.wait_ge(gates_ready, 1)
                        for part in range(2):
                            mm = pe.matmul(r_ps[0:KG[0], :], remap[:, part, :],
                                           gold[:, part, hf * HALF:(hf + 1) * HALF],
                                           start=part == 0, stop=part == 1, skip_group_check=True)
                        mm.then_inc(turned, 1)
                    return
                pe.wait_ge(gcat_ready, 1 + layer)
                kg = KG[layer]
                for hf in range(2):
                    if hf:
                        pe.wait_ge(gates_ready, 2 * layer + 1)
                    for i in range(TT // 2):
                        mm = pe.transpose(r_ps[0:kg, i * P:(i + 1) * P],
                                          gcat[:, hf * (TT // 2) + i, 0:kg].bitcast(F32), ident_s[:, :])
                    mm.then_inc(turned, 1)

            pe.wait_ge(in_rc, 7 * 16)
            for layer in range(NL):
                router(layer)

                def body(gs, c, k):
                    up(layer, gs, c, k)
                    if k == 0:
                        if layer == 0:
                            positions()
                        turn(layer)
                    gate(layer, gs, c, k)
                    if k:
                        down(layer, gs - 1, k - 1, k < 3)

                steps(pe, layer, body)
                down(layer, S0[layer] + 2 * CH[layer] - 1, 3, False)

        @block.scalar
        def _(act):
            def weights_hi(c, slot, glu):
                if glu:
                    act.wait_ge(raw_in[slot], (c - slot) * 8 + 16)
                    act.activation(w_hi[:, slot, :], raw[:, slot, :], ACT.Copy).then_inc(w_hi_ready, 1)
                else:
                    act.wait_ge(w_deq, c - GLU + 1)
                    act.activation(w_hi[:, slot, 0:2 * C], raw[:, slot, 0:2 * C], ACT.Copy
                                   ).then_inc(act_done, 1)
                    act.activation(w_hi[0:KG[3], slot, WC:WC + P], raw_sel[:, slot, :], ACT.Copy
                                   ).then_inc(w_hi_ready, 1)

            def cond_layer(layer):
                for n, (hf, m) in enumerate(BLOCKS):
                    if layer:
                        act.wait_ge(x_ready, 4 * (layer - 1) + n + 1)
                    elif n == 0:
                        act.wait_ge(in_x, 16)
                    act.activation(blk(cnd, hf, m), blk(x, hf, m), ACT.Sigmoid).then_inc(sig_ready, 1)
                for n, (hf, m) in enumerate(BLOCKS):
                    act.wait_ge(c_ready, 4 * layer + n + 1)
                    act.activation(blk(c_hi, hf, m), blk(cnd, hf, m), ACT.Copy).then_inc(c_hi_ready, 1)

            def router_act(layer):
                n = GW[layer]
                if layer == 2:
                    act.wait_ge(logits_ready, 4)
                    act.activation(lg[:, :, E2:2 * E2],
                                   r_ps[:, 0:TT * n].rearrange("p (i e) -> p i e", i=TT)[:, :, E2:2 * E2],
                                   ACT.Silu).then_inc(rexp, 1)
                    n = E2
                if layer == 3:
                    act.wait_ge(lgt, 4)
                    act.activation(sel[:, :, 0:n], lg[:, :, 0:n], ACT.Exp, scale=-1.0).then_inc(act_done, 1)
                    act.wait_ge(act_done, ACT_BEFORE_L3)
                    act.activation(ex[:, :, 0:n], sel[:, :, 0:n], ACT.Ln, bias=1.0).then_inc(rexp, 1)
                act.wait_ge(lgt, [1, 2, 3, 5][layer])
                act.activation(ex[:, :, 0:n], lg[:, :, 0:n], ACT.Exp).then_inc(rexp, 1)

            def turned_copy(layer):
                kg = KG[layer]
                if layer == 0:
                    yf = y_ps[:, :, :, :].rearrange("p a b n -> p (a b n)")
                    act.wait_ge(turned, 1)
                    for part in range(2):
                        for hf in range(2):
                            o = part * TOK + hf * HALF
                            act.activation(gold[:, part, hf * HALF:(hf + 1) * HALF], yf[:, o:o + HALF],
                                           ACT.Copy).then_inc(rexp, 1)
                for hf in range(2):
                    act.wait_ge(turned, 1 + 2 * layer + hf + 1)
                    act.activation(gates[0:kg, hf * HALF:(hf + 1) * HALF], r_ps[0:kg, :], ACT.Copy
                                   ).then_inc(gates_ready, 1)

            act.wait_ge(in_wu, 16)
            act.activation(wexp[:, :, :], wus[:, :, 0, :], ACT.Exp).then_inc(act_done, 1)
            act.wait_ge(act_done, 1)
            act.activation(wexp[:, :, :], wexp[:, :, :], ACT.Exp, scale=-1.0).then_inc(wexp_ready, 1)
            act.wait_ge(kexp_ready, 1)
            act.activation(ek[:, :, :], ek[:, :, :], ACT.Exp).then_inc(kexp_ready, 1)
            for layer in range(NL):
                act.wait_ge(uk_ready, layer + 1)
                q = slice(layer * UNITS, (layer + 1) * UNITS)
                act.activation(R[:, q, :], R[:, q, :], ACT.Exp).then_inc(euk_ready, 1)
            act.wait_ge(tf_ready, 1)
            act.activation(tf[:, :], tfs[:, :], ACT.Sigmoid).then_inc(tf_ready, 1)
            weights_hi(0, 0, True)
            ACT_BEFORE_L3 = 1 + 1 + 1
            for layer in range(NL):
                cond_layer(layer)
                router_act(layer)

                def body(gs, c, k):
                    par = k % 2
                    if k == 0:
                        turned_copy(layer)
                    act.wait_ge(g_ready, gs + 1)
                    wait(act, t_ready, gs - 1)
                    act.activation(act_g[:, par, :], g_ps[:, par, :], ACT.Silu if layer < 3 else ACT.Relu
                                   ).then_inc(act_ready, 1)
                    last = k == 2 * CH[layer] - 1
                    if par and not (last and layer == 3):
                        wait(act, y_done, gs - 1)
                        j = (k + 1) // 2
                        weights_hi(c + 1, j % 2, layer < 2 or (layer == 2 and not last))
                    act.wait_ge(h_ready, gs + 1)
                    wait(act, y_done, gs - 1)
                    act.activation(h_hi[:, par, :], h[:, par, :], ACT.Copy).then_inc(h_hi_ready, 1)

                steps(act, layer, body)

        @block.vector
        def _(dve):
            count = [0]

            def link(ins):
                count[0] += 1
                ins.then_inc(dve_done, 1)
                dve.wait_ge(dve_done, count[0])

            def scans(q, base, buf):
                dec = decay[:, bass.ds(base + q, 1)].to_broadcast([P, NT])
                for n, (src, rev) in enumerate(((ekv, ekv_rev), (ek, ek_rev))):
                    dve.tensor_tensor_scan(fwd[:, buf, n, :], dec, unit(src, q), 0.0, ALU.mult, ALU.add)
                    last = dve.tensor_tensor_scan(bwd[:, buf, n, ::-1], dec, unit(rev, q), 0.0,
                                                  ALU.mult, ALU.add)
                last.then_inc(scan_ready, 1)

            def ratio(q, base, done, buf):
                dve.wait_ge(num_ready, base + q + 1)
                den = fwd[:, buf, 1, :]
                dve.tensor_scalar(den, den, 1e-8, None, ALU.max).then_inc(done, 1)
                dve.wait_ge(done, (base + q) * 3 + 1)
                dve.reciprocal(den, den).then_inc(done, 1)
                dve.wait_ge(done, (base + q) * 3 + 2)
                dve.scalar_tensor_tensor(out=unit(R, base + q), in0=fwd[:, buf, 0, :],
                                         scalar=oscale[:, bass.ds(base + q, 1)], in1=den,
                                         op0=ALU.mult, op1=ALU.mult).then_inc(done, 1)
                dve.wait_ge(done, (base + q) * 3 + 3)

            dve.wait_ge(in_te, 16)
            dve.tensor_reduce(tfs[:, :], te[:, :, :], AX, ALU.add).then_inc(tf_ready, 1)
            dve.wait_ge(in_fs, 16)
            dve.tensor_scalar(ek[:, :, :], fs[:, :, :], 30.0, None, ALU.min).then_inc(kexp_ready, 1)
            dve.wait_ge(in_wu, 16)
            for layer in range(NL):
                for kt in range(KT):
                    q = layer * UNITS + kt * NB
                    ins = dve.tensor_scalar(R[:, q:q + NB, :], fs[:, kt * NB:(kt + 1) * NB, :],
                                            wus[:, layer, 1, kt:kt + 1], 30.0, ALU.add, ALU.min)
                ins.then_inc(uk_ready, 1)
            dve.wait_ge(kexp_ready, 2)
            link(dve.tensor_tensor(ekv[:, :, :], ek[:, :, :], fs[:, :, :], ALU.mult))
            dve.tensor_copy(ek_rev[:, :, ::-1], ek[:, :, :])
            link(dve.tensor_copy(ekv_rev[:, :, ::-1], ekv[:, :, :]))
            dve.wait_ge(tf_ready, 2)
            link(dve.tensor_scalar(tdec[:, :], tf[:, :], 0.5, 0.5, ALU.mult, ALU.add))
            dve.wait_ge(wexp_ready, 1)
            for layer in range(NL):
                for kt in range(KT):
                    q = layer * UNITS + kt * NB
                    dve.tensor_scalar(decay[:, q:q + NB], tdec[:, :], wexp[:, layer, kt:kt + 1], None,
                                      ALU.mult)
                    ins = dve.tensor_scalar(oscale[:, q:q + NB], tf[:, :], 0.2, 0.8, ALU.mult, ALU.add)
            link(ins)
            for layer in range(NL):
                with dve.Fori(0, UNITS // 2) as i:
                    for r in range(2):
                        scans(i * 2 + r, layer * UNITS, r)
                    for r in range(2):
                        ratio(i * 2 + r, layer * UNITS, R_ready, r)

            dve.wait_ge(in_rc, 7 * 16)
            dve.tensor_copy(tri16[:, :], tri_s[:, :])
            dve.memset(ones16[:, :], 1.0)
            dve.tensor_copy(o2n_c[:, :], o2n_ci[:, :])
            link(dve.tensor_copy(keep[:, 0, :], keep_i[:, :]))
            link(dve.tensor_scalar(keep[:, 0, :], keep[:, 0, :], -1.0, None, ALU.not_equal))
            dve.tensor_scalar(keep[:, 1, :], keep[:, 0, :], -1.0, 1e30, ALU.add, ALU.mult)
            for part in range(2):
                link(dve.memset(remap[:, part, :].bitcast(F32), 0.0))
                link(dve.tensor_scalar(remap[:, part, part * KEPT:(part + 1) * KEPT],
                                       iota_s[:, 0:KEPT], o2n_c[:, 0:1], None, ALU.is_equal))

            def cond_layer(layer):
                for n, (hf, m) in enumerate(BLOCKS):
                    dve.wait_ge(sig_ready, 4 * layer + n + 1)
                    q = layer * UNITS + m * NB + hf * NB // 2
                    dve.tensor_tensor(blk(cnd, hf, m), blk(cnd, hf, m),
                                      R[:, q:q + NB // 2, :].rearrange("p a n -> p (a n)"), ALU.mult
                                      ).then_inc(c_ready, 1)

            def spread(v, n):
                return v.unsqueeze(2).to_broadcast([P, TT, n])

            def softmax_parts(layer, src, n):
                link(dve.tensor_reduce(r8[:, 0, :], src, AX, ALU.max))
                dve.tensor_tensor(lg[:, :, 0:n], src, spread(r8[:, 0, :], n), ALU.subtract
                                  ).then_inc(lgt, 1)
                dve.wait_ge(rexp, [1, 6, 8, 10][layer])
                link(dve.tensor_reduce(r8[:, 1, :], ex[:, :, 0:n], AX, ALU.add))

            def top2(src, n):
                for i in range(TT):
                    ins = dve.max(v8[:, i, :], src[:, i, 0:n])
                link(ins)
                for i in range(TT):
                    ins = dve.max_index(i8[:, i, :], v8[:, i, :], src[:, i, 0:n])
                link(ins)
                link(dve.tensor_copy(if8[:, :, :], i8[:, :, 0:2]))
                io = iota_s[:, 0:n].unsqueeze(1).to_broadcast([P, TT, n])
                dve.tensor_tensor(sel[:, :, 0:n], io, if8[:, :, 0:1].to_broadcast([P, TT, n]),
                                  ALU.is_equal)
                link(dve.tensor_tensor(sel[:, :, 32:32 + n], io, if8[:, :, 1:2].to_broadcast([P, TT, n]),
                                       ALU.is_equal))
                link(dve.tensor_tensor(sel[:, :, 0:n], sel[:, :, 0:n], sel[:, :, 32:32 + n], ALU.add))

            def parts(g, n, one):
                if one:
                    link(dve.memset(g[:, :, n:n + 1], 1.0))
                    n += 1
                link(dve.tensor_copy(gcat[:, :, 0:n], g[:, :, 0:n]))
                dve.tensor_tensor(gcat[:, :, n:2 * n], g[:, :, 0:n], gcat[:, :, 0:n].bitcast(F32),
                                  ALU.subtract).then_inc(gcat_ready, 1)

            def magnitude(dst, src):
                return dve.scalar_tensor_tensor(out=dst, in0=src, scalar=-1.0, in1=src, op0=ALU.mult,
                                                op1=ALU.max)

            def router0():
                dve.wait_ge(logits_ready, 1)
                yl = y_ps[:, 0, :, :].rearrange("p a (i e) -> p (a i) e", e=E0)
                kb = keep[:, 0:1, :].to_broadcast([P, TT, E0])
                link(dve.tensor_tensor(lg[:, :, :], yl, kb, ALU.mult))
                link(dve.tensor_tensor(lg[:, :, :], lg[:, :, :],
                                       keep[:, 1:2, :].to_broadcast([P, TT, E0]), ALU.add))
                softmax_parts(0, lg[:, :, :], E0)
                for i in range(TT):
                    ins = dve.max(v8[:, i, :], ex[:, i, :])
                link(ins)
                for i in range(TT):
                    ins = dve.match_replace(lg[:, i, :], v8[:, i, :], ex[:, i, :], -1.0)
                link(ins)
                link(dve.tensor_scalar(sel[:, :, :], lg[:, :, :], 0.0, None, ALU.is_lt))
                dve.tensor_copy(sel16[:, :, :], sel[:, :, :]).then_inc(rpe, 1)
                link(dve.tensor_reduce(r8[:, 2, :], v8[:, :, :], AX, ALU.add))
                link(dve.reciprocal(r8[:, 3, :], r8[:, 2, :]))
                link(dve.tensor_tensor(ex[:, :, :], ex[:, :, :], sel[:, :, :], ALU.mult))
                link(dve.tensor_tensor(ex[:, :, :], ex[:, :, :], spread(r8[:, 3, :], E0), ALU.mult))
                dve.wait_ge(logits_ready, 2)
                yp = y_ps[:, 1, :, :].rearrange("p a (i e) -> p (a i) e", e=E0)
                link(dve.tensor_scalar(sel[:, :, :], yp, CAP - 0.5, None, ALU.is_lt))
                link(dve.tensor_tensor(ex[:, :, :], ex[:, :, :], sel[:, :, :], ALU.mult))
                link(dve.tensor_copy(gcat[:, :, :], ex[:, :, :]))
                dve.tensor_tensor(lg[:, :, :], ex[:, :, :], gcat[:, :, :].bitcast(F32), ALU.subtract
                                  ).then_inc(gcat_ready, 1)

            def router(layer):
                n = [E0, E1, E2, E3][layer]
                rp = r_ps[:, 0:TT * GW[layer]].rearrange("p (i e) -> p i e", i=TT)
                dve.wait_ge(logits_ready, layer + 2)
                if layer == 1:
                    softmax_parts(1, rp, n)
                    top2(ex, n)
                elif layer == 2:
                    dve.wait_ge(rexp, 7)
                    link(dve.tensor_tensor(lg[:, :, 0:n], rp[:, :, 0:n], lg[:, :, E2:2 * E2], ALU.mult))
                    link(magnitude(lg[:, :, 0:n], lg[:, :, 0:n]))
                    softmax_parts(2, lg[:, :, 0:n], n)
                    link(dve.reciprocal(r8[:, 3, :], r8[:, 1, :]))
                    link(dve.tensor_tensor(ex[:, :, 0:n], ex[:, :, 0:n], spread(r8[:, 3, :], n), ALU.mult))
                    link(dve.tensor_tensor(lg[:, :, 0:n], ex[:, :, 0:n],
                                           rcs[:, 1:2, :].to_broadcast([P, TT, n]), ALU.add))
                    top2(lg, n)
                    link(dve.tensor_tensor(ex[:, :, 0:n], ex[:, :, 0:n],
                                           rcs[:, 0:1, :].to_broadcast([P, TT, n]), ALU.mult))
                    link(dve.tensor_scalar(ex[:, :, 0:n], ex[:, :, 0:n], 1.0, None, ALU.add))
                    link(dve.tensor_tensor(ex[:, :, 0:n], ex[:, :, 0:n], sel[:, :, 0:n], ALU.mult))
                    parts(ex, n, True)
                    return
                else:
                    link(dve.tensor_scalar(ex[:, :, 32:32 + n], rp, 0.0, None, ALU.min))
                    link(dve.tensor_copy(lg[:, :, 64:64 + n], rp))
                    magnitude(lg[:, :, 0:n], lg[:, :, 64:64 + n]).then_inc(lgt, 1)
                    dve.wait_ge(rexp, 9)
                    link(dve.tensor_tensor(lg[:, :, 32:32 + n], ex[:, :, 32:32 + n], ex[:, :, 0:n],
                                           ALU.subtract))
                    softmax_parts(3, lg[:, :, 32:32 + n], n)
                    top2(ex, n)
                link(dve.tensor_tensor(ex[:, :, 0:n], ex[:, :, 0:n], sel[:, :, 0:n], ALU.mult))
                link(dve.tensor_reduce(r8[:, 2, :], ex[:, :, 0:n], AX, ALU.add))
                link(dve.scalar_tensor_tensor(out=r8[:, 2, :], in0=r8[:, 1, :], scalar=EPS,
                                              in1=r8[:, 2, :], op0=ALU.mult, op1=ALU.add))
                link(dve.reciprocal(r8[:, 3, :], r8[:, 2, :]))
                link(dve.tensor_tensor(ex[:, :, 0:n], ex[:, :, 0:n], spread(r8[:, 3, :], n), ALU.mult))
                parts(ex, n, layer == 1)

            def dequantize(e, slot, use16):
                dve.wait_ge(q_in[slot], use16)
                w = raw[:, slot, 0:2 * C]
                dve.wait_ge(w_lo_ready, e + (GLU - 1))
                dve.scalar_tensor_tensor(out=w, in0=raw_q[:, slot, :], scalar=-8.0,
                                         in1=raw_s[:, slot, :], op0=ALU.add, op1=ALU.mult
                                         ).then_inc(w_deq_part, 1)
                dve.wait_ge(w_deq_part, e * 2 + 1)
                dve.tensor_scalar(raw[:, slot, 0:C], raw[:, slot, 0:C], gsc[:, 0:1], None, ALU.mult
                                  ).then_inc(w_deq_part, 1)
                dve.tensor_scalar(raw[:, slot, C:2 * C], raw[:, slot, C:2 * C], gsc[:, 1:2], None,
                                  ALU.mult).then_inc(w_deq, 1)

            for layer in range(NL):
                cond_layer(layer)
                if layer == 0:
                    router0()
                else:
                    router(layer)

                def body(gs, c, k):
                    par = k % 2
                    dve.wait_ge(act_ready, gs + 1)
                    if layer < 3:
                        dve.wait_ge(u_ready, gs + 1)
                        dve.tensor_tensor(t[:, par, :], act_g[:, par, :], u_ps[:, :], ALU.mult
                                          ).then_inc(t_ready, 1)
                    else:
                        dve.tensor_tensor(t[:, par, :], act_g[:, par, :], act_g[:, par, :], ALU.mult
                                          ).then_inc(t_ready, 1)
                    last = k == 2 * CH[layer] - 1
                    if layer == 2 and last:
                        dequantize(0, 0, 16 * QLOADS)
                    if layer == 3 and par and not last:
                        j = (k + 1) // 2
                        e = c + (1 - GLU)
                        dequantize(e, j % 2, (e - j % 2) * (8 * QLOADS) + 16 * QLOADS)
                    dve.wait_ge(t_ready, gs + 1)
                    dve.wait_ge(gate_ready, gs + 1)
                    wait(dve, h_lo_ready, gs - 1)
                    gate_ps = g_ps[:, par, :] if layer < 3 else u_ps[:, :]
                    dve.tensor_tensor(h[:, par, :], t[:, par, :], gate_ps, ALU.mult).then_inc(h_ready, 1)

                steps(dve, layer, body)
                for n, (hf, m) in enumerate(BLOCKS):
                    dve.wait_ge(y_done, S0[layer] + 2 * CH[layer] - 1 + hf)
                    dve.tensor_tensor(blk(x, hf, m), blk(x, hf, m), y_ps[:, m, hf, :], ALU.add
                                      ).then_inc(x_ready, 1)

        @block.gpsimd
        def _(pool):
            def lo_part(dst, src, hi):
                return pool.tensor_tensor(dst, src, hi.bitcast(F32), ALU.subtract)

            def weights_lo(c, slot, n):
                pool.wait_ge(w_hi_ready, c + 1)
                lo_part(w_lo[:, slot, 0:n], raw[:, slot, 0:n], w_hi[:, slot, 0:n]).then_inc(w_lo_ready, 1)

            def wkv_dif(q, base, buf):
                e, dv, d = unit(R, base + q), dif[:, buf, 0, :], dif[:, buf, 1, :]
                pool.tensor_tensor(d, e, unit(ek, q), ALU.subtract).then_inc(dif_ready, 1)
                pool.wait_ge(dif_ready, (base + q) * 2 + 1)
                pool.tensor_tensor(dv, d, unit(fs, q), ALU.mult).then_inc(dif_ready, 1)

            def wkv_sum(q, base, buf):
                pool.wait_ge(scan_ready, base + q + 1)
                pool.wait_ge(dif_ready, (base + q) * 2 + 2)
                s = fwd[:, buf, :, :].rearrange("p f n -> p (f n)")
                pool.tensor_tensor(s, s, bwd[:, buf, :, :].rearrange("p f n -> p (f n)"), ALU.add
                                   ).then_inc(sum_ready, 1)
                pool.wait_ge(sum_ready, base + q + 1)
                pool.tensor_tensor(s, s, dif[:, buf, :, :].rearrange("p f n -> p (f n)"), ALU.add
                                   ).then_inc(num_ready, 1)

            for layer in range(NL):
                pool.wait_ge(euk_ready, layer + 1)
                with pool.Fori(0, UNITS // 2) as i:
                    for r in range(2):
                        wkv_dif(i * 2 + r, layer * UNITS, r)
                    for r in range(2):
                        wkv_sum(i * 2 + r, layer * UNITS, r)
            weights_lo(0, 0, WC)
            for layer in range(NL):
                for n, (hf, m) in enumerate(BLOCKS):
                    pool.wait_ge(c_hi_ready, 4 * layer + n + 1)
                    lo_part(blk(c_lo, hf, m), blk(cnd, hf, m), blk(c_hi, hf, m)).then_inc(c_lo_ready, 1)

                def body(gs, c, k):
                    par = k % 2
                    last = k == 2 * CH[layer] - 1
                    if par and not (last and layer == 3):
                        weights_lo(c + 1, ((k + 1) // 2) % 2,
                                   WC if layer < 2 or (layer == 2 and not last) else 2 * C)
                    pool.wait_ge(h_hi_ready, gs + 1)
                    lo_part(h_lo[:, par, :], h[:, par, :], h_hi[:, par, :]).then_inc(h_lo_ready, 1)

                steps(pool, layer, body)


def constants():
    import numpy as np
    sels = []
    for n_exp, inter, shared, chunks in ((KEPT, I0, 0, CH[0]), (E1, I1, SH1, CH[1]), (E2, I2, SH2, CH[2])):
        rows = n_exp + (shared > 0)
        s = np.zeros((P, chunks * P), np.float32)
        for e in range(n_exp + (shared > 0)):
            cols = slice(e * inter, (e + 1) * inter) if e < n_exp else slice(e * inter, e * inter + shared)
            s[e, cols] = 1.0
            s[rows + e, cols] = 1.0
        sels.append(s.reshape(P, chunks, P).transpose(1, 0, 2))
    sel3 = np.zeros((E3, KG[3], P), np.float32)
    for e in range(E3):
        sel3[e, [e, E3 + e], :] = 1.0
    tri = np.triu(np.ones((P, P), np.float32), 1)
    iota = np.tile(np.arange(E0, dtype=np.float32), (P, 1))
    return np.concatenate(sels), sel3, np.eye(P, dtype=np.float32), tri, iota


def pack_glu(gate, up, down, chunks):
    import numpy as np
    pad = chunks * P - gate.shape[1]
    gate, up = (np.pad(a, ((0, 0), (0, pad))) for a in (gate, up))
    down = np.pad(down, ((0, pad), (0, 0)))
    gu = [a.reshape(KT, P, chunks, P).transpose(2, 1, 0, 3).reshape(chunks, P, KT * P) for a in (gate, up)]
    return np.concatenate(gu + [down.reshape(chunks, P, C)], axis=2)


def kernel(**inputs):
    import numpy as np
    import concourse.bacc as bacc
    from concourse import mybir as _mybir
    from concourse.bass_utils import run_bass_kernel_spmd

    a = {k: np.asarray(v) for k, v in inputs.items()}
    sels, sel3, ident, tri, iota = constants()

    def rows(w):
        return w.reshape(-1, C).T

    def cols(w):
        return w.transpose(0, 2, 1).reshape(-1, C)

    gu = a["L0_ffn_gate_up_proj"]
    packs = [pack_glu(rows(gu[:, :I0]), rows(gu[:, I0:]), cols(a["L0_ffn_down_proj"]), CH[0])]
    flat = {n: a["L1_ffn_" + n].transpose(1, 0, 2).reshape(C, -1) for n in ("wg", "wu")}
    packs.append(pack_glu(np.concatenate([flat["wg"], a["L1_ffn_sg"]], 1),
                          np.concatenate([flat["wu"], a["L1_ffn_su"]], 1),
                          np.concatenate([a["L1_ffn_wd"].reshape(-1, C), a["L1_ffn_sd"]], 0), CH[1]))
    packs.append(pack_glu(np.concatenate([rows(a["L2_ffn_wg"]), rows(a["L2_ffn_sg"])], 1),
                          np.concatenate([rows(a["L2_ffn_wu"]), rows(a["L2_ffn_su"])], 1),
                          np.concatenate([cols(a["L2_ffn_wd"]), a["L2_ffn_sd"].T], 0), CH[2]))
    up_q = a["L3_ffn_fc_up_qweights"].reshape(E3, KT, P, I3).transpose(0, 2, 1, 3).reshape(E3, P, C)
    gw = np.concatenate([a["L0_ffn_gate_weight"], a["L1_ffn_router_w"], a["L2_ffn_cls_w"],
                         a["L2_ffn_gate_w"], a["L3_ffn_gate_weight"]], 0)
    wu = np.stack([np.stack([a[f"L{l}_cond_{n}"] for n in "wu"]) for l in range(NL)])
    arrays = {
        "xT": a["x"].reshape(TOK, C).T.reshape(KT, P, TOK),
        "fT": a["fside_BxSxS_0"].reshape(TOK, C).T.reshape(KT, P, TOK),
        "cond": a["cond_512"].reshape(1, NB * TD),
        "wu": wu.reshape(NL * 2 * KT, P).T,
        "o2n_row": a["L0_ffn_old_to_new"].reshape(1, E0),
        "o2n_col": a["L0_ffn_old_to_new"].reshape(E0, 1),
        "gwT": gw.T.reshape(KT, P, -1).transpose(1, 0, 2),
        "rconst": np.concatenate([a["L2_ffn_extra_scale"], a["L2_ffn_extra_bias"]]).reshape(1, -1),
        "gscale": np.concatenate([a["L3_ffn_fc_up_global_scale"],
                                  a["L3_ffn_fc_down_global_scale"]]).reshape(1, 2),
        "wglu": np.concatenate([np.concatenate(packs, 0), sels], 2),
        "wq": np.concatenate([up_q, a["L3_ffn_fc_down_qweights"]], 2),
        "s_up": a["L3_ffn_fc_up_blocks_scale"],
        "s_down": a["L3_ffn_fc_down_blocks_scale"],
        "sel3": sel3, "ident": ident, "tri": tri, "iota": iota,
    }
    nc = bacc.Bacc("TRN2", target_bir_lowering=False, num_devices=1)
    arrays = {f"in_{k}": np.ascontiguousarray(v) for k, v in arrays.items()}
    aps = [nc.dram_tensor(k, v.shape, _mybir.dt.from_np(v.dtype), kind="ExternalInput").ap()
           for k, v in arrays.items()]
    out = nc.dram_tensor("out", (KT, P, TOK), F32, kind="ExternalOutput").ap()
    build(nc, *aps, out)
    r = run_bass_kernel_spmd(nc, [arrays], core_ids=[0])
    return r.results[0]["out"].reshape(C, TOK).T.reshape(NB, NT, C)
```

```python
from contextlib import ExitStack

import concourse.bass as bass
from concourse import mybir

P = 128
NB, NT, C = 4, 256, 256
TOK = NB * NT
KT = C // P
HALF = TOK // 2
TT = TOK // P
NL = 4
TD = 64
UNITS = KT * NB
WKV_TRIPS = UNITS // 2
HB = 4

E0, KEPT, TOP0, CAP, I0 = 128, 48, 8, 96, 96
E1, I1, SH1 = 8, 176, 352
E2, I2, SH2 = 14, 176, 352
E3, I3, GROUP = 16, 128, 16
EPS = 1e-20

CH = [KEPT * I0 // P, -(-(E1 * I1 + SH1) // P), (E2 * I2 + SH2) // P, E3]
C0 = [sum(CH[:l]) for l in range(NL)]
S0 = [2 * c for c in C0]
GLU = C0[3]
KG = [2 * KEPT, 2 * (E1 + 1), 2 * (E2 + 1), 2 * E3]
UPC = 2 * KT * P
DN0 = UPC + P
WC = DN0 + C
GW = [E0, E1, 2 * E2, E3]
G0 = [sum(GW[:l]) for l in range(NL)]
NG = P // GROUP
QLOADS = 2 + KT + 1
assert all(c % 2 == 0 for c in CH)

F32, F32R, BF16, I32, U32 = (mybir.dt.float32, mybir.dt.float32r, mybir.dt.bfloat16,
                             mybir.dt.int32, mybir.dt.uint32)
ALU = mybir.AluOpType
ACT = mybir.ActivationFunctionType
AX = mybir.AxisListType.X


def wait(eng, sem, value):
    if not isinstance(value, int) or value > 0:
        eng.wait_ge(sem, value)


def steps(eng, layer, body, behind=None):
    s0, c0, n = S0[layer], C0[layer], 2 * CH[layer]
    for k in range(4):
        body(s0 + k, c0 + k // 2, k)
    split = 1 + (WKV_TRIPS if behind else 0)
    if behind:
        with eng.Fori(1, split) as i:
            for k in range(4):
                body(i * 4 + (s0 + k), i * 2 + (c0 + k // 2), k + 4)
                behind(i * 2 - 2, k)
    with eng.Fori(split, n // 4 - 1) as i:
        for k in range(4):
            body(i * 4 + (s0 + k), i * 2 + (c0 + k // 2), k + 4)
    for k in range(n - 4, n):
        body(s0 + k, c0 + k // 2, k)


def build(nc, xT, fT, cond, wu, o2n_row, o2n_col, gwT, rconst, gscale, wglu, wq, s_up, s_down, sel3,
          ident, tri, iota, out):
    with ExitStack() as ctx:
        def sb(name, shape, dt=F32):
            return ctx.enter_context(nc.sbuf_tensor(name, shape, dt))

        def sem(name):
            return ctx.enter_context(nc.semaphore(name))

        x = sb("x", [P, KT, TOK])
        cnd = sb("cnd", [P, KT, TOK])
        c_hi = sb("c_hi", [P, KT, TOK], F32R)
        c_lo = sb("c_lo", [P, KT, TOK], F32R)
        R = sb("R", [P, NL * UNITS, NT])
        fs = sb("fs", [P, UNITS, NT])
        ek = sb("ek", [P, UNITS, NT])
        ekv = sb("ekv", [P, UNITS, NT])
        ek_rev = sb("ek_rev", [P, UNITS, NT])
        ekv_rev = sb("ekv_rev", [P, UNITS, NT])
        fwd = sb("fwd", [P, 2, 2, NT])
        bwd = sb("bwd", [P, 2, 2, NT])
        dif = sb("dif", [P, 2, 2, NT])
        te = sb("te", [P, NB, TD])
        tfs = sb("tfs", [P, NB])
        tf = sb("tf", [P, NB])
        tdec = sb("tdec", [P, NB])
        wus = sb("wus", [P, NL, 2, KT])
        wexp = sb("wexp", [P, NL, KT])
        decay = sb("decay", [P, NL * UNITS])
        oscale = sb("oscale", [P, NL * UNITS])
        raw = sb("raw", [P, 2, WC])
        raw_q = sb("raw_q", [P, 2, 2 * C], I32)
        raw_s = sb("raw_s", [P, 2, 2 * C])
        raw_sel = sb("raw_sel", [KG[3], 2, P])
        w_hi = sb("w_hi", [P, 2, WC], F32R)
        w_lo = sb("w_lo", [P, 2, WC], F32R)
        act_g = sb("act_g", [P, 2, HALF])
        t = sb("t", [P, 2, HALF])
        h = sb("h", [P, 2, HALF])
        h_hi = sb("h_hi", [P, HB, HALF], F32R)
        h_lo = sb("h_lo", [P, HB, HALF], F32R)
        gws = sb("gws", [P, KT, sum(GW)])
        gates = sb("gates", [P, TOK], F32R)
        lg = sb("lg", [P, TT, E0])
        ex = sb("ex", [P, TT, E0])
        sel = sb("sel", [P, TT, E0])
        sel16 = sb("sel16", [P, TT, E0], BF16)
        gcat = sb("gcat", [P, TT, E0], F32R)
        gold = h_hi[:, :, :].rearrange("p (a b) n -> p a (b n)", a=2)
        v8 = sb("v8", [P, TT, 8])
        i8 = sb("i8", [P, TT, 8], U32)
        if8 = sb("if8", [P, TT, 2])
        r8 = sb("r8", [P, 4, TT])
        rcs = sb("rcs", [P, 2, E2])
        gsc = sb("gsc", [P, 2])
        keep_i = sb("keep_i", [P, E0], I32)
        keep = sb("keep", [P, 2, E0])
        o2n_ci = sb("o2n_ci", [P, 1], I32)
        o2n_c = sb("o2n_c", [P, 1])
        remap = sb("remap", [P, 2, 2 * KEPT], F32R)
        ident_s = sb("ident_s", [P, P])
        tri_s = sb("tri_s", [P, P])
        tri16 = sb("tri16", [P, P], BF16)
        ones16 = sb("ones16", [P, P], BF16)
        iota_s = sb("iota_s", [P, E0])

        y_ps = ctx.enter_context(nc.psum_tensor("y_ps", [P, KT, 2, HALF], F32))
        g_ps = ctx.enter_context(nc.psum_tensor("g_ps", [P, 2, HALF], F32))
        u_ps = ctx.enter_context(nc.psum_tensor("u_ps", [P, HALF], F32))
        r_ps = ctx.enter_context(nc.psum_tensor("r_ps", [P, 512], F32))

        in_x, in_fs, in_te, in_wu = sem("in_x"), sem("in_fs"), sem("in_te"), sem("in_wu")
        in_gw, in_rc = sem("in_gw"), sem("in_rc")
        raw_in = [sem("raw_in0"), sem("raw_in1")]
        q_in = [sem("q_in0"), sem("q_in1")]
        up_hi_ready, up_lo_ready, w_deq = sem("up_hi_ready"), sem("up_lo_ready"), sem("w_deq")
        down_hi_ready, down_lo_ready = sem("down_hi_ready"), sem("down_lo_ready")
        w_deq_part, sum_ready = sem("w_deq_part"), sem("sum_ready")
        g_ready, u_ready, gate_ready = sem("g_ready"), sem("u_ready"), sem("gate_ready")
        act_ready, t_ready, h_ready = sem("act_ready"), sem("t_ready"), sem("h_ready")
        h_hi_ready, h_lo_ready, y_done = sem("h_hi_ready"), sem("h_lo_ready"), sem("y_done")
        x_ready, sig_ready, c_ready = sem("x_ready"), sem("sig_ready"), sem("c_ready")
        c_hi_ready, c_lo_ready = sem("c_hi_ready"), sem("c_lo_ready")
        logits_ready, lgt, rexp, rpe, gcat_ready = (sem("logits_ready"), sem("lgt"), sem("rexp"),
                                                    sem("rpe"), sem("gcat_ready"))
        turned, gates_ready = sem("turned"), sem("gates_ready")
        dve_done, act_done = sem("dve_done"), sem("act_done")
        tf_ready, kexp_ready, ekv_ready = sem("tf_ready"), sem("kexp_ready"), sem("ekv_ready")
        uk_ready, euk_ready, wexp_ready = sem("uk_ready"), sem("euk_ready"), sem("wexp_ready")
        dif_ready, scan_ready, num_ready, R_ready = (sem("dif_ready"), sem("scan_ready"),
                                                     sem("num_ready"), sem("R_ready"))
        out_done = sem("out_done")

        block = ctx.enter_context(nc.Block())

        BLOCKS = [(hf, m) for hf in range(2) for m in range(KT)]

        def blk(tensor, hf, m):
            return tensor[:, m, hf * HALF:(hf + 1) * HALF]

        def unit(tensor, q):
            return tensor[:, bass.ds(q, 1), :].rearrange("p a n -> p (a n)")

        @block.sync
        def _(sp):
            def load_glu(c, slot):
                wait(sp, down_lo_ready, c - 1)
                sp.dma_start(raw[:, slot, :], wglu[bass.ds(c, 1)].rearrange("a p n -> p (a n)")
                             ).then_inc(raw_in[slot], 16)

            sp.dma_start(fs[:, :, :].rearrange("p (k b) n -> p k (b n)", k=KT),
                         fT.rearrange("k p n -> p k n")).then_inc(in_fs, 16)
            sp.dma_start(te[:, :, :].rearrange("p b n -> p (b n)"), cond.to_broadcast([P, NB * TD])
                         ).then_inc(in_te, 16)
            sp.dma_start(wus[:, :, :, :].rearrange("p a b c -> p (a b c)"), wu).then_inc(in_wu, 16)
            sp.dma_start(x[:, :, :], xT.rearrange("k p n -> p k n")).then_inc(in_x, 16)
            for dst, src in ((keep_i[:, :], o2n_row.to_broadcast([P, E0])), (o2n_ci[:, :], o2n_col),
                             (rcs[:, :, :].rearrange("p a n -> p (a n)"),
                              rconst.to_broadcast([P, 2 * E2])),
                             (gsc[:, :], gscale.to_broadcast([P, 2])),
                             (ident_s[:, :], ident), (tri_s[:, :], tri), (iota_s[:, :], iota)):
                sp.dma_start(dst, src).then_inc(in_rc, 16)
            sp.dma_start(gws[:, :, :], gwT).then_inc(in_gw, 16)
            load_glu(0, 0)
            load_glu(1, 1)
            with sp.Fori(1, GLU // 2) as i:
                load_glu(i * 2, 0)
                load_glu(i * 2 + 1, 1)

            def load_q(e, slot):
                ex_ = slice(e, e + 1) if isinstance(e, int) else bass.ds(e, 1)
                sp.dma_start(raw_q[:, slot, :], wq[ex_].rearrange("a p n -> p (a n)")
                             ).then_inc(q_in[slot], 16)
                for k in range(KT + 1):
                    src = s_up[ex_, k * NG:(k + 1) * NG, :] if k < KT else s_down[ex_]
                    cols = slice(k * P, (k + 1) * P) if k < KT else slice(C, 2 * C)
                    n = src.shape[2]
                    src = src.rearrange("a g n -> (a g) n").unsqueeze(1).to_broadcast([NG, GROUP, n])
                    sp.dma_start(raw_s[:, slot, cols], src
                                 ).then_inc(q_in[slot], 16)
                sp.dma_start(raw_sel[:, slot, :], sel3[ex_].rearrange("a p n -> p (a n)")
                             ).then_inc(q_in[slot], 16)

            load_q(0, 0)
            load_q(1, 1)
            with sp.Fori(1, E3 // 2) as i:
                for slot in range(2):
                    sp.wait_ge(down_lo_ready, i * 2 + (GLU + slot - 1))
                    load_q(i * 2 + slot, slot)
            for n, (hf, m) in enumerate(BLOCKS):
                sp.wait_ge(x_ready, (NL - 1) * len(BLOCKS) + n + 1)
                sp.dma_start(out[m, :, hf * HALF:(hf + 1) * HALF], blk(x, hf, m)).then_inc(out_done, 16)
            sp.wait_ge(out_done, 16 * len(BLOCKS))

        @block.tensor
        def _(pe):
            def split_mm(dst, w_at, rhs_hi, rhs_lo, start, stop):
                n = 0
                for slot, cols, k in w_at:
                    for w, r in ((w_hi, rhs_hi), (w_hi, rhs_lo), (w_lo, rhs_hi)):
                        n += 1
                        mm = pe.matmul(dst, w[:, slot, cols], r(k), start=start and n == 1,
                                       stop=stop and n == 3 * len(w_at), skip_group_check=True)
                return mm

            def up(layer, gs, c, k):
                hf, par, slot = k % 2, k % 2, (k // 2) % 2
                tok = slice(hf * HALF, (hf + 1) * HALF)

                def col(j):
                    return slice(j * P, (j + 1) * P)

                def hi(kt):
                    return c_hi[:, kt, tok]

                def lo(kt):
                    return c_lo[:, kt, tok]

                if hf == 0:
                    pe.wait_ge(up_lo_ready, c + 1)
                if k < 2:
                    pe.wait_ge(c_lo_ready, 4 * layer + 2 * hf + 2)
                wait(pe, h_ready, gs - 1)
                split_mm(g_ps[:, par, :], [(slot, col(j), j) for j in range(KT)], hi, lo,
                         True, True).then_inc(g_ready, 1)
                if layer < 3:
                    wait(pe, t_ready, gs)
                    split_mm(u_ps[:, :], [(slot, col(KT + j), j) for j in range(KT)], hi, lo,
                             True, True).then_inc(u_ready, 1)

            def gate(layer, gs, c, k):
                hf, par, slot = k % 2, k % 2, (k // 2) % 2
                tok = slice(hf * HALF, (hf + 1) * HALF)
                if k < 1:
                    pe.wait_ge(gates_ready, 2 * layer + 2)
                wait(pe, act_ready, gs + 1)
                if layer == 3:
                    wait(pe, h_ready, gs)
                pe.matmul(g_ps[:, par, :] if layer < 3 else u_ps[:, :],
                          w_hi[0:KG[layer], slot, UPC:DN0], gates[0:KG[layer], tok],
                          start=True, stop=True, skip_group_check=True).then_inc(gate_ready, 1)

            def down(gs, c, k, start):
                hf, slot = k % 2, (k // 2) % 2
                if hf == 0:
                    pe.wait_ge(down_lo_ready, c + 1)
                pe.wait_ge(h_lo_ready, gs + 1)
                for m in range(KT):
                    mm = split_mm(y_ps[:, m, hf, :], [(slot, slice(DN0 + m * P, DN0 + (m + 1) * P), 0)],
                                  lambda _: h_hi[:, k % HB, :], lambda _: h_lo[:, k % HB, :], start,
                                  False)
                mm.then_inc(y_done, 1)

            def logits(layer, dst, tiles, n0):
                for i in tiles:
                    for kt in range(KT):
                        mm = pe.matmul(dst(i), cnd[:, kt, i * P:(i + 1) * P],
                                       gws[:, kt, G0[layer]:G0[layer] + GW[layer]],
                                       start=kt == 0, stop=kt == KT - 1, skip_group_check=True)
                return mm

            def router(layer):
                pe.wait_ge(c_ready, 4 * layer + 4)
                if layer == 0:
                    pe.wait_ge(in_gw, 16)
                n = GW[layer]
                if layer:
                    logits(layer, lambda i: r_ps[:, i * n:(i + 1) * n], range(TT), 0
                           ).then_inc(logits_ready, 1)
                else:
                    yf = y_ps[:, 0, :, :].rearrange("p a n -> p (a n)")
                    logits(0, lambda i: yf[:, i * n:(i + 1) * n], range(TT), 0).then_inc(logits_ready, 1)

            def positions():
                pos = y_ps[:, 1, :, :].rearrange("p a n -> p (a n)")
                pe.wait_ge(rpe, 1)
                for i in range(TT):
                    for j in range(i + 1):
                        mm = pe.matmul(pos[:, i * E0:(i + 1) * E0],
                                       (tri16 if j == i else ones16)[:, :], sel16[:, j, :],
                                       start=j == 0, stop=j == i, skip_group_check=True)
                mm.then_inc(logits_ready, 1)

            def turn(layer):
                if layer == 0:
                    yf = y_ps[:, :, :, :].rearrange("p a b n -> p (a b n)")
                    pe.wait_ge(gcat_ready, 1)
                    gh = [gcat[:, :, :].bitcast(F32), lg[:, :, :]]
                    for part in range(2):
                        for i in range(TT):
                            mm = pe.transpose(yf[:, part * TOK + i * P:part * TOK + (i + 1) * P],
                                              gh[part][:, i, :], ident_s[:, :])
                    mm.then_inc(turned, 1)
                    pe.wait_ge(rexp, 5)
                    for hf in range(2):
                        if hf:
                            pe.wait_ge(gates_ready, 1)
                        for part in range(2):
                            mm = pe.matmul(r_ps[0:KG[0], :], remap[:, part, :],
                                           gold[:, part, hf * HALF:(hf + 1) * HALF],
                                           start=part == 0, stop=part == 1, skip_group_check=True)
                        mm.then_inc(turned, 1)
                    return
                pe.wait_ge(gcat_ready, 1 + layer)
                kg = KG[layer]
                for hf in range(2):
                    if hf:
                        pe.wait_ge(gates_ready, 2 * layer + 1)
                    for i in range(TT // 2):
                        mm = pe.transpose(r_ps[0:kg, i * P:(i + 1) * P],
                                          gcat[:, hf * (TT // 2) + i, 0:kg].bitcast(F32), ident_s[:, :])
                    mm.then_inc(turned, 1)

            pe.wait_ge(in_rc, 7 * 16)
            for layer in range(NL):
                router(layer)

                def body(gs, c, k):
                    up(layer, gs, c, k)
                    if k == 0:
                        if layer == 0:
                            positions()
                        turn(layer)
                    gate(layer, gs, c, k)
                    if k >= 2:
                        down(gs - 2, c - 1, k - 2, k < 4)

                steps(pe, layer, body)
                for k in (2, 3):
                    down(S0[layer] + 2 * CH[layer] - 4 + k, C0[layer] + CH[layer] - 1, k, False)

        @block.scalar
        def _(act):
            def up_hi(c, slot, glu):
                if glu:
                    act.wait_ge(raw_in[slot], (c - slot) * 8 + 16)
                    act.activation(w_hi[:, slot, 0:DN0], raw[:, slot, 0:DN0], ACT.Copy
                                   ).then_inc(up_hi_ready, 1)
                else:
                    act.wait_ge(w_deq, c - GLU + 1)
                    act.activation(w_hi[:, slot, 0:C], raw[:, slot, 0:C], ACT.Copy)
                    act.activation(w_hi[0:KG[3], slot, UPC:DN0], raw_sel[:, slot, :], ACT.Copy
                                   ).then_inc(up_hi_ready, 1)

            def down_hi(slot):
                act.activation(w_hi[:, slot, DN0:WC], raw[:, slot, DN0:WC], ACT.Copy
                               ).then_inc(down_hi_ready, 1)

            def cond_layer(layer):
                for n, (hf, m) in enumerate(BLOCKS):
                    if layer:
                        act.wait_ge(x_ready, 4 * (layer - 1) + n + 1)
                    elif n == 0:
                        act.wait_ge(in_x, 16)
                    act.activation(blk(cnd, hf, m), blk(x, hf, m), ACT.Sigmoid).then_inc(sig_ready, 1)
                for n, (hf, m) in enumerate(BLOCKS):
                    act.wait_ge(c_ready, 4 * layer + n + 1)
                    act.activation(blk(c_hi, hf, m), blk(cnd, hf, m), ACT.Copy).then_inc(c_hi_ready, 1)

            def router_act(layer):
                n = GW[layer]
                if layer == 2:
                    act.wait_ge(logits_ready, 4)
                    act.activation(lg[:, :, E2:2 * E2],
                                   r_ps[:, 0:TT * n].rearrange("p (i e) -> p i e", i=TT)[:, :, E2:2 * E2],
                                   ACT.Silu).then_inc(rexp, 1)
                    n = E2
                if layer == 3:
                    act.wait_ge(lgt, 4)
                    act.activation(sel[:, :, 0:n], lg[:, :, 0:n], ACT.Exp, scale=-1.0).then_inc(act_done, 1)
                    act.wait_ge(act_done, 2)
                    act.activation(ex[:, :, 0:n], sel[:, :, 0:n], ACT.Ln, bias=1.0).then_inc(rexp, 1)
                act.wait_ge(lgt, [1, 2, 3, 5][layer])
                act.activation(ex[:, :, 0:n], lg[:, :, 0:n], ACT.Exp).then_inc(rexp, 1)

            def turned_copy(layer):
                kg = KG[layer]
                if layer == 0:
                    yf = y_ps[:, :, :, :].rearrange("p a b n -> p (a b n)")
                    act.wait_ge(turned, 1)
                    for part in range(2):
                        for hf in range(2):
                            o = part * TOK + hf * HALF
                            act.activation(gold[:, part, hf * HALF:(hf + 1) * HALF], yf[:, o:o + HALF],
                                           ACT.Copy).then_inc(rexp, 1)
                for hf in range(2):
                    act.wait_ge(turned, 1 + 2 * layer + hf + 1)
                    act.activation(gates[0:kg, hf * HALF:(hf + 1) * HALF], r_ps[0:kg, :], ACT.Copy
                                   ).then_inc(gates_ready, 1)

            act.wait_ge(in_wu, 16)
            act.activation(wexp[:, :, :], wus[:, :, 0, :], ACT.Exp).then_inc(act_done, 1)
            act.wait_ge(act_done, 1)
            act.activation(wexp[:, :, :], wexp[:, :, :], ACT.Exp, scale=-1.0).then_inc(wexp_ready, 1)
            act.wait_ge(kexp_ready, 1)
            act.activation(ek[:, :, :], ek[:, :, :], ACT.Exp).then_inc(kexp_ready, 1)
            for layer in range(NL):
                act.wait_ge(uk_ready, layer + 1)
                q = slice(layer * UNITS, (layer + 1) * UNITS)
                act.activation(R[:, q, :], R[:, q, :], ACT.Exp).then_inc(euk_ready, 1)
            act.wait_ge(tf_ready, 1)
            act.activation(tf[:, :], tfs[:, :], ACT.Sigmoid).then_inc(tf_ready, 1)
            up_hi(0, 0, True)
            for layer in range(NL):
                cond_layer(layer)
                router_act(layer)

                def body(gs, c, k):
                    par = k % 2
                    if k == 0:
                        turned_copy(layer)
                    act.wait_ge(g_ready, gs + 1)
                    wait(act, t_ready, gs - 1)
                    act.activation(act_g[:, par, :], g_ps[:, par, :], ACT.Silu if layer < 3 else ACT.Relu
                                   ).then_inc(act_ready, 1)
                    slot = (k // 2) % 2
                    if par:
                        wait(act, y_done, gs - 3)
                        down_hi(slot)
                    act.wait_ge(h_ready, gs + 1)
                    wait(act, y_done, gs - 3)
                    act.activation(h_hi[:, k % HB, :], h[:, par, :], ACT.Copy).then_inc(h_hi_ready, 1)
                    last = k == 2 * CH[layer] - 2
                    if not par and not (last and layer == 3):
                        wait(act, gate_ready, gs)
                        up_hi(c + 1, 1 - slot, layer < 2 or (layer == 2 and not last))

                steps(act, layer, body)

        @block.vector
        def _(dve):
            count = [0]

            def link(ins):
                count[0] += 1
                ins.then_inc(dve_done, 1)
                dve.wait_ge(dve_done, count[0])

            def scans(q, base, buf):
                dec = decay[:, bass.ds(base + q, 1)].to_broadcast([P, NT])
                for n, (src, rev) in enumerate(((ekv, ekv_rev), (ek, ek_rev))):
                    dve.tensor_tensor_scan(fwd[:, buf, n, :], dec, unit(src, q), 0.0, ALU.mult, ALU.add)
                    last = dve.tensor_tensor_scan(bwd[:, buf, n, ::-1], dec, unit(rev, q), 0.0,
                                                  ALU.mult, ALU.add)
                last.then_inc(scan_ready, 1)

            def ratio(q, base, buf):
                dve.wait_ge(num_ready, base + q + 1)
                den = fwd[:, buf, 1, :]
                dve.tensor_scalar(den, den, 1e-8, None, ALU.max).then_inc(R_ready, 1)
                dve.wait_ge(R_ready, (base + q) * 3 + 1)
                dve.reciprocal(den, den).then_inc(R_ready, 1)
                dve.wait_ge(R_ready, (base + q) * 3 + 2)
                dve.scalar_tensor_tensor(out=unit(R, base + q), in0=fwd[:, buf, 0, :],
                                         scalar=oscale[:, bass.ds(base + q, 1)], in1=den,
                                         op0=ALU.mult, op1=ALU.mult).then_inc(R_ready, 1)
                dve.wait_ge(R_ready, (base + q) * 3 + 3)

            dve.wait_ge(in_te, 16)
            dve.tensor_reduce(tfs[:, :], te[:, :, :], AX, ALU.add).then_inc(tf_ready, 1)
            dve.wait_ge(in_fs, 16)
            dve.tensor_scalar(ek[:, :, :], fs[:, :, :], 30.0, None, ALU.min).then_inc(kexp_ready, 1)
            dve.wait_ge(in_wu, 16)
            for layer in range(NL):
                for kt in range(KT):
                    q = layer * UNITS + kt * NB
                    ins = dve.tensor_scalar(R[:, q:q + NB, :], fs[:, kt * NB:(kt + 1) * NB, :],
                                            wus[:, layer, 1, kt:kt + 1], 30.0, ALU.add, ALU.min)
                ins.then_inc(uk_ready, 1)
            dve.wait_ge(kexp_ready, 2)
            link(dve.tensor_tensor(ekv[:, :, :], ek[:, :, :], fs[:, :, :], ALU.mult))
            dve.tensor_copy(ek_rev[:, :, ::-1], ek[:, :, :])
            link(dve.tensor_copy(ekv_rev[:, :, ::-1], ekv[:, :, :]))
            dve.wait_ge(tf_ready, 2)
            link(dve.tensor_scalar(tdec[:, :], tf[:, :], 0.5, 0.5, ALU.mult, ALU.add))
            dve.wait_ge(wexp_ready, 1)
            for layer in range(NL):
                for kt in range(KT):
                    q = layer * UNITS + kt * NB
                    dve.tensor_scalar(decay[:, q:q + NB], tdec[:, :], wexp[:, layer, kt:kt + 1], None,
                                      ALU.mult)
                    ins = dve.tensor_scalar(oscale[:, q:q + NB], tf[:, :], 0.2, 0.8, ALU.mult, ALU.add)
            link(ins)
            with dve.Fori(0, UNITS // 2) as i:
                for r in range(2):
                    scans(i * 2 + r, 0, r)
                for r in range(2):
                    ratio(i * 2 + r, 0, r)

            dve.wait_ge(in_rc, 7 * 16)
            dve.tensor_copy(tri16[:, :], tri_s[:, :])
            dve.memset(ones16[:, :], 1.0)
            dve.tensor_copy(o2n_c[:, :], o2n_ci[:, :])
            link(dve.tensor_copy(keep[:, 0, :], keep_i[:, :]))
            link(dve.tensor_scalar(keep[:, 0, :], keep[:, 0, :], -1.0, None, ALU.not_equal))
            dve.tensor_scalar(keep[:, 1, :], keep[:, 0, :], -1.0, 1e30, ALU.add, ALU.mult)
            for part in range(2):
                link(dve.memset(remap[:, part, :].bitcast(F32), 0.0))
                link(dve.tensor_scalar(remap[:, part, part * KEPT:(part + 1) * KEPT],
                                       iota_s[:, 0:KEPT], o2n_c[:, 0:1], None, ALU.is_equal))

            def cond_layer(layer):
                for n, (hf, m) in enumerate(BLOCKS):
                    dve.wait_ge(sig_ready, 4 * layer + n + 1)
                    q = layer * UNITS + m * NB + hf * NB // 2
                    dve.tensor_tensor(blk(cnd, hf, m), blk(cnd, hf, m),
                                      R[:, q:q + NB // 2, :].rearrange("p a n -> p (a n)"), ALU.mult
                                      ).then_inc(c_ready, 1)

            def spread(v, n):
                return v.unsqueeze(2).to_broadcast([P, TT, n])

            def softmax_parts(layer, src, n):
                link(dve.tensor_reduce(r8[:, 0, :], src, AX, ALU.max))
                dve.tensor_tensor(lg[:, :, 0:n], src, spread(r8[:, 0, :], n), ALU.subtract
                                  ).then_inc(lgt, 1)
                dve.wait_ge(rexp, [1, 6, 8, 10][layer])
                link(dve.tensor_reduce(r8[:, 1, :], ex[:, :, 0:n], AX, ALU.add))

            def top2(src, n):
                for i in range(TT):
                    ins = dve.max(v8[:, i, :], src[:, i, 0:n])
                link(ins)
                for i in range(TT):
                    ins = dve.max_index(i8[:, i, :], v8[:, i, :], src[:, i, 0:n])
                link(ins)
                link(dve.tensor_copy(if8[:, :, :], i8[:, :, 0:2]))
                io = iota_s[:, 0:n].unsqueeze(1).to_broadcast([P, TT, n])
                dve.tensor_tensor(sel[:, :, 0:n], io, if8[:, :, 0:1].to_broadcast([P, TT, n]),
                                  ALU.is_equal)
                link(dve.tensor_tensor(sel[:, :, 32:32 + n], io, if8[:, :, 1:2].to_broadcast([P, TT, n]),
                                       ALU.is_equal))
                link(dve.tensor_tensor(sel[:, :, 0:n], sel[:, :, 0:n], sel[:, :, 32:32 + n], ALU.add))

            def parts(g, n, one):
                if one:
                    link(dve.memset(g[:, :, n:n + 1], 1.0))
                    n += 1
                link(dve.tensor_copy(gcat[:, :, 0:n], g[:, :, 0:n]))
                dve.tensor_tensor(gcat[:, :, n:2 * n], g[:, :, 0:n], gcat[:, :, 0:n].bitcast(F32),
                                  ALU.subtract).then_inc(gcat_ready, 1)

            def magnitude(dst, src):
                return dve.scalar_tensor_tensor(out=dst, in0=src, scalar=-1.0, in1=src, op0=ALU.mult,
                                                op1=ALU.max)

            def router0():
                dve.wait_ge(logits_ready, 1)
                yl = y_ps[:, 0, :, :].rearrange("p a (i e) -> p (a i) e", e=E0)
                kb = keep[:, 0:1, :].to_broadcast([P, TT, E0])
                link(dve.tensor_tensor(lg[:, :, :], yl, kb, ALU.mult))
                link(dve.tensor_tensor(lg[:, :, :], lg[:, :, :],
                                       keep[:, 1:2, :].to_broadcast([P, TT, E0]), ALU.add))
                softmax_parts(0, lg[:, :, :], E0)
                for i in range(TT):
                    ins = dve.max(v8[:, i, :], ex[:, i, :])
                link(ins)
                for i in range(TT):
                    ins = dve.match_replace(lg[:, i, :], v8[:, i, :], ex[:, i, :], -1.0)
                link(ins)
                link(dve.tensor_scalar(sel[:, :, :], lg[:, :, :], 0.0, None, ALU.is_lt))
                dve.tensor_copy(sel16[:, :, :], sel[:, :, :]).then_inc(rpe, 1)
                link(dve.tensor_reduce(r8[:, 2, :], v8[:, :, :], AX, ALU.add))
                link(dve.reciprocal(r8[:, 3, :], r8[:, 2, :]))
                link(dve.tensor_tensor(ex[:, :, :], ex[:, :, :], sel[:, :, :], ALU.mult))
                link(dve.tensor_tensor(ex[:, :, :], ex[:, :, :], spread(r8[:, 3, :], E0), ALU.mult))
                dve.wait_ge(logits_ready, 2)
                yp = y_ps[:, 1, :, :].rearrange("p a (i e) -> p (a i) e", e=E0)
                link(dve.tensor_scalar(sel[:, :, :], yp, CAP - 0.5, None, ALU.is_lt))
                link(dve.tensor_tensor(ex[:, :, :], ex[:, :, :], sel[:, :, :], ALU.mult))
                link(dve.tensor_copy(gcat[:, :, :], ex[:, :, :]))
                dve.tensor_tensor(lg[:, :, :], ex[:, :, :], gcat[:, :, :].bitcast(F32), ALU.subtract
                                  ).then_inc(gcat_ready, 1)

            def router(layer):
                n = [E0, E1, E2, E3][layer]
                rp = r_ps[:, 0:TT * GW[layer]].rearrange("p (i e) -> p i e", i=TT)
                dve.wait_ge(logits_ready, layer + 2)
                if layer == 1:
                    softmax_parts(1, rp, n)
                    top2(ex, n)
                elif layer == 2:
                    dve.wait_ge(rexp, 7)
                    link(dve.tensor_tensor(lg[:, :, 0:n], rp[:, :, 0:n], lg[:, :, E2:2 * E2], ALU.mult))
                    link(magnitude(lg[:, :, 0:n], lg[:, :, 0:n]))
                    softmax_parts(2, lg[:, :, 0:n], n)
                    link(dve.reciprocal(r8[:, 3, :], r8[:, 1, :]))
                    link(dve.tensor_tensor(ex[:, :, 0:n], ex[:, :, 0:n], spread(r8[:, 3, :], n), ALU.mult))
                    link(dve.tensor_tensor(lg[:, :, 0:n], ex[:, :, 0:n],
                                           rcs[:, 1:2, :].to_broadcast([P, TT, n]), ALU.add))
                    top2(lg, n)
                    link(dve.tensor_tensor(ex[:, :, 0:n], ex[:, :, 0:n],
                                           rcs[:, 0:1, :].to_broadcast([P, TT, n]), ALU.mult))
                    link(dve.tensor_scalar(ex[:, :, 0:n], ex[:, :, 0:n], 1.0, None, ALU.add))
                    link(dve.tensor_tensor(ex[:, :, 0:n], ex[:, :, 0:n], sel[:, :, 0:n], ALU.mult))
                    parts(ex, n, True)
                    return
                else:
                    link(dve.tensor_scalar(ex[:, :, 32:32 + n], rp, 0.0, None, ALU.min))
                    link(dve.tensor_copy(lg[:, :, 64:64 + n], rp))
                    magnitude(lg[:, :, 0:n], lg[:, :, 64:64 + n]).then_inc(lgt, 1)
                    dve.wait_ge(rexp, 9)
                    link(dve.tensor_tensor(lg[:, :, 32:32 + n], ex[:, :, 32:32 + n], ex[:, :, 0:n],
                                           ALU.subtract))
                    softmax_parts(3, lg[:, :, 32:32 + n], n)
                    top2(ex, n)
                link(dve.tensor_tensor(ex[:, :, 0:n], ex[:, :, 0:n], sel[:, :, 0:n], ALU.mult))
                link(dve.tensor_reduce(r8[:, 2, :], ex[:, :, 0:n], AX, ALU.add))
                link(dve.scalar_tensor_tensor(out=r8[:, 2, :], in0=r8[:, 1, :], scalar=EPS,
                                              in1=r8[:, 2, :], op0=ALU.mult, op1=ALU.add))
                link(dve.reciprocal(r8[:, 3, :], r8[:, 2, :]))
                link(dve.tensor_tensor(ex[:, :, 0:n], ex[:, :, 0:n], spread(r8[:, 3, :], n), ALU.mult))
                parts(ex, n, layer == 1)

            def dequantize(e, slot):
                dve.wait_ge(q_in[slot], (e - slot) * (8 * QLOADS) + 16 * QLOADS)
                dve.wait_ge(down_lo_ready, e + (GLU - 1))
                up, dn = raw[:, slot, 0:C], raw[:, slot, DN0:WC]
                dve.scalar_tensor_tensor(out=up, in0=raw_q[:, slot, 0:C], scalar=-8.0,
                                         in1=raw_s[:, slot, 0:C], op0=ALU.add, op1=ALU.mult)
                dve.scalar_tensor_tensor(out=dn, in0=raw_q[:, slot, C:2 * C], scalar=-8.0,
                                         in1=raw_s[:, slot, C:2 * C], op0=ALU.add, op1=ALU.mult
                                         ).then_inc(w_deq_part, 1)
                dve.wait_ge(w_deq_part, e * 2 + 1)
                dve.tensor_scalar(up, up, gsc[:, 0:1], None, ALU.mult).then_inc(w_deq_part, 1)
                dve.tensor_scalar(dn, dn, gsc[:, 1:2], None, ALU.mult).then_inc(w_deq, 1)

            def weights_lo(slot, cols, hi_sem, lo_sem, c):
                dve.wait_ge(hi_sem, c + 1)
                dve.tensor_tensor(w_lo[:, slot, cols], raw[:, slot, cols],
                                  w_hi[:, slot, cols].bitcast(F32), ALU.subtract).then_inc(lo_sem, 1)

            def wkv(base):
                def behind(q, k):
                    if k < 2:
                        scans(q + k, base, k)
                    else:
                        ratio(q + (k - 2), base, k - 2)
                return behind

            weights_lo(0, slice(0, UPC), up_hi_ready, up_lo_ready, 0)
            for layer in range(NL):
                cond_layer(layer)
                if layer == 0:
                    router0()
                else:
                    router(layer)

                def body(gs, c, k):
                    par, slot, n = k % 2, (k // 2) % 2, 2 * CH[layer]
                    if par and not (k == n - 1 and layer == 3):
                        weights_lo(1 - slot, slice(0, UPC if layer < 2 or (layer == 2 and k < n - 1) else C),
                                   up_hi_ready, up_lo_ready, c + 1)
                    dve.wait_ge(act_ready, gs + 1)
                    if layer < 3:
                        dve.wait_ge(u_ready, gs + 1)
                        dve.tensor_tensor(t[:, par, :], act_g[:, par, :], u_ps[:, :], ALU.mult
                                          ).then_inc(t_ready, 1)
                    else:
                        dve.tensor_tensor(t[:, par, :], act_g[:, par, :], act_g[:, par, :], ALU.mult
                                          ).then_inc(t_ready, 1)
                    dve.wait_ge(t_ready, gs + 1)
                    dve.wait_ge(gate_ready, gs + 1)
                    wait(dve, h_lo_ready, gs - 1)
                    gate_ps = g_ps[:, par, :] if layer < 3 else u_ps[:, :]
                    dve.tensor_tensor(h[:, par, :], t[:, par, :], gate_ps, ALU.mult).then_inc(h_ready, 1)
                    if par:
                        weights_lo(slot, slice(DN0, WC), down_hi_ready, down_lo_ready, c)
                        if (layer == 2 and k >= n - 3) or (layer == 3 and k < n - 4):
                            dequantize(c + (2 - GLU), slot)

                steps(dve, layer, body, wkv((layer + 1) * UNITS) if layer < 3 else None)
                for n, (hf, m) in enumerate(BLOCKS):
                    dve.wait_ge(y_done, S0[layer] + 2 * CH[layer] - 1 + hf)
                    dve.tensor_tensor(blk(x, hf, m), blk(x, hf, m), y_ps[:, m, hf, :], ALU.add
                                      ).then_inc(x_ready, 1)

        @block.gpsimd
        def _(pool):
            def lo_part(dst, src, hi):
                return pool.tensor_tensor(dst, src, hi.bitcast(F32), ALU.subtract)

            def wkv_dif(q, base, buf):
                e, dv, d = unit(R, base + q), dif[:, buf, 0, :], dif[:, buf, 1, :]
                pool.tensor_tensor(d, e, unit(ek, q), ALU.subtract).then_inc(dif_ready, 1)
                pool.wait_ge(dif_ready, (base + q) * 2 + 1)
                pool.tensor_tensor(dv, d, unit(fs, q), ALU.mult).then_inc(dif_ready, 1)

            def wkv_sum(q, base, buf):
                pool.wait_ge(scan_ready, base + q + 1)
                pool.wait_ge(dif_ready, (base + q) * 2 + 2)
                s = fwd[:, buf, :, :].rearrange("p f n -> p (f n)")
                pool.tensor_tensor(s, s, bwd[:, buf, :, :].rearrange("p f n -> p (f n)"), ALU.add
                                   ).then_inc(sum_ready, 1)
                pool.wait_ge(sum_ready, base + q + 1)
                pool.tensor_tensor(s, s, dif[:, buf, :, :].rearrange("p f n -> p (f n)"), ALU.add
                                   ).then_inc(num_ready, 1)

            def wkv(base):
                def behind(q, k):
                    if k < 2:
                        wkv_dif(q + k, base, k)
                    if k in (1, 2):
                        wkv_sum(q + (k - 1), base, k - 1)
                return behind

            pool.wait_ge(euk_ready, NL)
            with pool.Fori(0, UNITS // 2) as i:
                for r in range(2):
                    wkv_dif(i * 2 + r, 0, r)
                for r in range(2):
                    wkv_sum(i * 2 + r, 0, r)
            for layer in range(NL):
                for n, (hf, m) in enumerate(BLOCKS):
                    pool.wait_ge(c_hi_ready, 4 * layer + n + 1)
                    lo_part(blk(c_lo, hf, m), blk(cnd, hf, m), blk(c_hi, hf, m)).then_inc(c_lo_ready, 1)

                def body(gs, c, k):
                    pool.wait_ge(h_hi_ready, gs + 1)
                    lo_part(h_lo[:, k % HB, :], h[:, k % 2, :], h_hi[:, k % HB, :]).then_inc(h_lo_ready, 1)

                steps(pool, layer, body, wkv((layer + 1) * UNITS) if layer < 3 else None)


def constants():
    import numpy as np
    sels = []
    for n_exp, inter, shared, chunks in ((KEPT, I0, 0, CH[0]), (E1, I1, SH1, CH[1]), (E2, I2, SH2, CH[2])):
        rows = n_exp + (shared > 0)
        s = np.zeros((P, chunks * P), np.float32)
        for e in range(n_exp + (shared > 0)):
            cols = slice(e * inter, (e + 1) * inter) if e < n_exp else slice(e * inter, e * inter + shared)
            s[e, cols] = 1.0
            s[rows + e, cols] = 1.0
        sels.append(s.reshape(P, chunks, P).transpose(1, 0, 2))
    sel3 = np.zeros((E3, KG[3], P), np.float32)
    for e in range(E3):
        sel3[e, [e, E3 + e], :] = 1.0
    tri = np.triu(np.ones((P, P), np.float32), 1)
    iota = np.tile(np.arange(E0, dtype=np.float32), (P, 1))
    return sels, sel3, np.eye(P, dtype=np.float32), tri, iota


def pack_glu(gate, up, down, sel, chunks):
    import numpy as np
    pad = chunks * P - gate.shape[1]
    gate, up = (np.pad(a, ((0, 0), (0, pad))) for a in (gate, up))
    down = np.pad(down, ((0, pad), (0, 0)))
    gu = [a.reshape(KT, P, chunks, P).transpose(2, 1, 0, 3).reshape(chunks, P, KT * P) for a in (gate, up)]
    return np.concatenate(gu + [sel, down.reshape(chunks, P, C)], axis=2)


def kernel(**inputs):
    import numpy as np
    import concourse.bacc as bacc
    from concourse import mybir as _mybir
    from concourse.bass_utils import run_bass_kernel_spmd

    a = {k: np.asarray(v) for k, v in inputs.items()}
    sels, sel3, ident, tri, iota = constants()

    def rows(w):
        return w.reshape(-1, C).T

    def cols(w):
        return w.transpose(0, 2, 1).reshape(-1, C)

    gu = a["L0_ffn_gate_up_proj"]
    packs = [pack_glu(rows(gu[:, :I0]), rows(gu[:, I0:]), cols(a["L0_ffn_down_proj"]), sels[0], CH[0])]
    flat = {n: a["L1_ffn_" + n].transpose(1, 0, 2).reshape(C, -1) for n in ("wg", "wu")}
    packs.append(pack_glu(np.concatenate([flat["wg"], a["L1_ffn_sg"]], 1),
                          np.concatenate([flat["wu"], a["L1_ffn_su"]], 1),
                          np.concatenate([a["L1_ffn_wd"].reshape(-1, C), a["L1_ffn_sd"]], 0), sels[1], CH[1]))
    packs.append(pack_glu(np.concatenate([rows(a["L2_ffn_wg"]), rows(a["L2_ffn_sg"])], 1),
                          np.concatenate([rows(a["L2_ffn_wu"]), rows(a["L2_ffn_su"])], 1),
                          np.concatenate([cols(a["L2_ffn_wd"]), a["L2_ffn_sd"].T], 0), sels[2], CH[2]))
    up_q = a["L3_ffn_fc_up_qweights"].reshape(E3, KT, P, I3).transpose(0, 2, 1, 3).reshape(E3, P, C)
    gw = np.concatenate([a["L0_ffn_gate_weight"], a["L1_ffn_router_w"], a["L2_ffn_cls_w"],
                         a["L2_ffn_gate_w"], a["L3_ffn_gate_weight"]], 0)
    wu = np.stack([np.stack([a[f"L{l}_cond_{n}"] for n in "wu"]) for l in range(NL)])
    arrays = {
        "xT": a["x"].reshape(TOK, C).T.reshape(KT, P, TOK),
        "fT": a["fside_BxSxS_0"].reshape(TOK, C).T.reshape(KT, P, TOK),
        "cond": a["cond_512"].reshape(1, NB * TD),
        "wu": wu.reshape(NL * 2 * KT, P).T,
        "o2n_row": a["L0_ffn_old_to_new"].reshape(1, E0),
        "o2n_col": a["L0_ffn_old_to_new"].reshape(E0, 1),
        "gwT": gw.T.reshape(KT, P, -1).transpose(1, 0, 2),
        "rconst": np.concatenate([a["L2_ffn_extra_scale"], a["L2_ffn_extra_bias"]]).reshape(1, -1),
        "gscale": np.concatenate([a["L3_ffn_fc_up_global_scale"],
                                  a["L3_ffn_fc_down_global_scale"]]).reshape(1, 2),
        "wglu": np.concatenate(packs, 0),
        "wq": np.concatenate([up_q, a["L3_ffn_fc_down_qweights"]], 2),
        "s_up": a["L3_ffn_fc_up_blocks_scale"],
        "s_down": a["L3_ffn_fc_down_blocks_scale"],
        "sel3": sel3, "ident": ident, "tri": tri, "iota": iota,
    }
    nc = bacc.Bacc("TRN2", target_bir_lowering=False, num_devices=1)
    arrays = {f"in_{k}": np.ascontiguousarray(v) for k, v in arrays.items()}
    aps = [nc.dram_tensor(k, v.shape, _mybir.dt.from_np(v.dtype), kind="ExternalInput").ap()
           for k, v in arrays.items()]
    out = nc.dram_tensor("out", (KT, P, TOK), F32, kind="ExternalOutput").ap()
    build(nc, *aps, out)
    r = run_bass_kernel_spmd(nc, [arrays], core_ids=[0])
    return r.results[0]["out"].reshape(C, TOK).T.reshape(NB, NT, C)
```

```python
from contextlib import ExitStack

import concourse.bass as bass
from concourse import mybir

P = 128
NB, NT, C = 4, 256, 256
TOK = NB * NT
KT = C // P
HALF = TOK // 2
TT = TOK // P
NL = 4
TD = 64
UNITS = KT * NB
WKV_IN = [(UNITS, 12), (UNITS + 12, 5), (UNITS + 17, 7), (0, 0)]
assert sum(n for _, n in WKV_IN) == (NL - 1) * UNITS
HB = 4

E0, KEPT, CAP, I0 = 128, 48, 96, 96
E1, I1, SH1 = 8, 176, 352
E2, I2, SH2 = 14, 176, 352
E3, I3, GROUP = 16, 128, 16
EPS = 1e-20

CH = [KEPT * I0 // P, -(-(E1 * I1 + SH1) // P), (E2 * I2 + SH2) // P, E3]
LEAD = 10
HEAD = [2 * LEAD, 4, 4, 4]
C0 = [LEAD + sum(CH[:l]) for l in range(NL)]
S0 = [2 * sum(CH[:l]) for l in range(NL)]
GLU = C0[3]
KG = [2 * KEPT, 2 * (E1 + 1), 2 * (E2 + 1), 2 * E3]
UPC = 2 * KT * P
DN0 = UPC + P
WC = DN0 + C
GW = [E0, E1, 2 * E2, E3]
G0 = [sum(GW[:l]) for l in range(NL)]
NG = P // GROUP
QLOADS = 2 + KT + 1
assert all(c % 2 == 0 for c in CH)

F32, F32R, BF16, I32 = mybir.dt.float32, mybir.dt.float32r, mybir.dt.bfloat16, mybir.dt.int32
ALU = mybir.AluOpType
ACT = mybir.ActivationFunctionType
AX = mybir.AxisListType.X


def wait(eng, sem, value):
    if not isinstance(value, int) or value > 0:
        eng.wait_ge(sem, value)


def place(layer, k):
    if layer == 0 and k < 2 * LEAD:
        return k - LEAD, k // LEAD
    if (k < 4 and layer) or (k >= 2 * CH[layer] - 4 and layer < NL - 1):
        return k // 4 * 2 + k % 2, k % 4 // 2
    return k // 2, k % 2


def firsts(layer):
    return (0, LEAD if layer == 0 else 2)


def single(layer, k):
    return layer == 0 and k < 2 * LEAD


def steps(eng, layer, body, behind=None, more=0):
    s0, c0, n, head = S0[layer], C0[layer], 2 * CH[layer], HEAD[layer] + more
    for k in range(head):
        body(s0 + k, c0 + place(layer, k)[0], k)
    q0, units = WKV_IN[layer]
    first, end = head // 4, n // 4 - 1
    split = first + (units if behind else 0)
    if split > first:
        with eng.Fori(first, split) as i:
            for k in range(4):
                body(i * 4 + (s0 + k), i * 2 + (c0 + k // 2), head + k)
                behind(i + (q0 - first), k)
    if split < end:
        with eng.Fori(split, end) as i:
            for k in range(4):
                body(i * 4 + (s0 + k), i * 2 + (c0 + k // 2), head + k)
    for k in range(n - 4, n):
        body(s0 + k, c0 + place(layer, k)[0], k)


def build(nc, xT, fT, cond, wu, o2n_row, o2n_col, gwT, rconst, gscale, wglu, wq, s_up, s_down, sel3,
          ident, tri, iota, out):
    with ExitStack() as ctx:
        def sb(name, shape, dt=F32):
            return ctx.enter_context(nc.sbuf_tensor(name, shape, dt))

        def sem(name):
            return ctx.enter_context(nc.semaphore(name))

        x = sb("x", [P, KT, TOK])
        cnd = sb("cnd", [P, KT, TOK])
        c_hi = sb("c_hi", [P, KT, TOK], F32R)
        c_lo = sb("c_lo", [P, KT, TOK], F32R)
        R = sb("R", [P, NL * UNITS, NT])
        fs = sb("fs", [P, UNITS, NT])
        ek = sb("ek", [P, UNITS, NT])
        ekv = sb("ekv", [P, UNITS, NT])
        ek_rev = sb("ek_rev", [P, UNITS, NT])
        ekv_rev = sb("ekv_rev", [P, UNITS, NT])
        fwd = sb("fwd", [P, 2, 2, NT])
        bwd = sb("bwd", [P, 2, 2, NT])
        dif = sb("dif", [P, 2, 2, NT])
        te = sb("te", [P, NB, TD])
        tfs = sb("tfs", [P, NB])
        tf = sb("tf", [P, NB])
        tdec = sb("tdec", [P, NB])
        wus = sb("wus", [P, NL, 2, KT])
        wexp = sb("wexp", [P, NL, KT])
        decay = sb("decay", [P, NL * UNITS])
        oscale = sb("oscale", [P, NL * UNITS])
        raw = sb("raw", [P, 2, WC])
        raw_q = sb("raw_q", [P, 2, 2 * C], I32)
        raw_s = sb("raw_s", [P, 2, 2 * C])
        raw_sel = sb("raw_sel", [KG[3], 2, P])
        w_hi = sb("w_hi", [P, 2, WC], F32R)
        w_lo = sb("w_lo", [P, 2, WC], F32R)
        act_g = sb("act_g", [P, 2, HALF])
        t = sb("t", [P, 2, HALF])
        h = sb("h", [P, 2, HALF])
        h_hi = sb("h_hi", [P, HB, HALF], F32R)
        h_lo = sb("h_lo", [P, HB, HALF], F32R)
        gws = sb("gws", [P, KT, sum(GW)])
        gates = sb("gates", [P, TOK], F32R)
        lg = sb("lg", [P, TT, E0])
        ex = sb("ex", [P, TT, E0])
        sel16 = sb("sel16", [P, TT, E0], BF16)
        gcat = sb("gcat", [P, TT, E0], F32R)
        gold = sb("gold", [P, 2, HALF], F32R)
        v8 = sb("v8", [P, TT, 8])
        top = sb("top", [P, TT, E3])
        r8 = sb("r8", [P, 4, TT])
        rcs = sb("rcs", [P, 2, E2])
        gsc = sb("gsc", [P, 2])
        keep_i = sb("keep_i", [P, E0], I32)
        keep = sb("keep", [P, 2, E0])
        o2n_ci = sb("o2n_ci", [P, 1], I32)
        o2n_c = sb("o2n_c", [P, 1])
        remap = sb("remap", [P, 2, 2 * KEPT], F32R)
        ident_s = sb("ident_s", [P, P])
        tri_s = sb("tri_s", [P, P])
        tri16 = sb("tri16", [P, P], BF16)
        ones16 = sb("ones16", [P, P], BF16)
        iota_s = sb("iota_s", [P, E0])

        y_ps = ctx.enter_context(nc.psum_tensor("y_ps", [P, KT, 2, HALF], F32))
        g_ps = ctx.enter_context(nc.psum_tensor("g_ps", [P, 2, HALF], F32))
        u_ps = ctx.enter_context(nc.psum_tensor("u_ps", [P, HALF], F32))
        r_ps = ctx.enter_context(nc.psum_tensor("r_ps", [P, 512], F32))

        in_x, in_te, in_wu = sem("in_x"), sem("in_te"), sem("in_wu")
        in_fs = [sem("in_fs0"), sem("in_fs1")]
        in_gw, in_rc = sem("in_gw"), sem("in_rc")
        raw_up_in = [sem("raw_up_in0"), sem("raw_up_in1")]
        raw_down_in = [sem("raw_down_in0"), sem("raw_down_in1")]
        q_in = [sem("q_in0"), sem("q_in1")]
        up_hi_ready, up_lo_ready, w_deq = sem("up_hi_ready"), sem("up_lo_ready"), sem("w_deq")
        down_hi_ready, down_lo_ready = sem("down_hi_ready"), sem("down_lo_ready")
        w_deq_part, sum_ready = sem("w_deq_part"), sem("sum_ready")
        g_ready, u_ready, gate_ready = sem("g_ready"), sem("u_ready"), sem("gate_ready")
        act_ready, t_ready, h_ready = sem("act_ready"), sem("t_ready"), sem("h_ready")
        h_hi_ready, h_lo_ready, y_done = sem("h_hi_ready"), sem("h_lo_ready"), sem("y_done")
        x_ready, sig_ready, c_ready = sem("x_ready"), sem("sig_ready"), sem("c_ready")
        c_hi_ready, c_lo_ready = sem("c_hi_ready"), sem("c_lo_ready")
        logits_ready, lgt, rexp, rpe, gcat_ready = (sem("logits_ready"), sem("lgt"), sem("rexp"),
                                                    sem("rpe"), sem("gcat_ready"))
        turned, gates_ready, gold_ready = sem("turned"), sem("gates_ready"), sem("gold_ready")
        dve_done, act_done = sem("dve_done"), sem("act_done")
        tf_ready, kmin_ready = sem("tf_ready"), sem("kmin_ready")
        ek_ready, ek_rev_ready = sem("ek_ready"), sem("ek_rev_ready")
        uk_ready, euk_ready, wexp_ready = sem("uk_ready"), sem("euk_ready"), sem("wexp_ready")
        dif_ready, scan_ready, num_ready, R_ready = (sem("dif_ready"), sem("scan_ready"),
                                                     sem("num_ready"), sem("R_ready"))
        out_done = sem("out_done")

        block = ctx.enter_context(nc.Block())

        BLOCKS = [(hf, m) for hf in range(2) for m in range(KT)]

        def blk(tensor, hf, m):
            return tensor[:, m, hf * HALF:(hf + 1) * HALF]

        def of_half(hf):
            return slice(hf * TT // 2, (hf + 1) * TT // 2)

        def batches(tensor, hf):
            return tensor[:, 0:UNITS, :].rearrange("p (k b) n -> p k (b n)", k=KT
                                                   )[:, :, hf * HALF:(hf + 1) * HALF]

        def half_units(hf, kt):
            return slice(kt * NB + hf * NB // 2, kt * NB + (hf + 1) * NB // 2)

        UNIT0 = [kt * NB + hf * NB // 2 + b for hf in range(2) for kt in range(KT) for b in range(NB // 2)]

        def unit(tensor, q):
            return tensor[:, bass.ds(q, 1), :].rearrange("p a n -> p (a n)")

        @block.sync
        def _(sp):
            def load_up(u, c, slot):
                wait(sp, up_lo_ready, u - 1)
                sp.dma_start(raw[:, slot, 0:DN0], wglu[bass.ds(c, 1), :, 0:DN0].rearrange("a p n -> p (a n)")
                             ).then_inc(raw_up_in[slot], 16)

            def load_down(u, c, slot):
                wait(sp, down_lo_ready, u - 1)
                sp.dma_start(raw[:, slot, DN0:WC],
                             wglu[bass.ds(c, 1), :, DN0:WC].rearrange("a p n -> p (a n)")
                             ).then_inc(raw_down_in[slot], 16)

            def load_pair(u, c, c_next):
                load_up(u + 1, c + 1, 1)
                load_down(u, c, 0)
                if c_next is not None:
                    load_up(u + 2, c_next, 0)
                load_down(u + 1, c + 1, 1)

            sp.dma_start(batches(fs, 0), fT.rearrange("k p n -> p k n")[:, :, 0:HALF]).then_inc(in_fs[0], 16)
            sp.dma_start(te[:, :, :].rearrange("p b n -> p (b n)"), cond.to_broadcast([P, NB * TD])
                         ).then_inc(in_te, 16)
            sp.dma_start(wus[:, :, :, :].rearrange("p a b c -> p (a b c)"), wu).then_inc(in_wu, 16)
            sp.dma_start(batches(fs, 1), fT.rearrange("k p n -> p k n")[:, :, HALF:TOK]
                         ).then_inc(in_fs[1], 16)
            sp.dma_start(x[:, :, :], xT.rearrange("k p n -> p k n")).then_inc(in_x, 16)
            for dst, src in ((keep_i[:, :], o2n_row.to_broadcast([P, E0])), (o2n_ci[:, :], o2n_col),
                             (rcs[:, :, :].rearrange("p a n -> p (a n)"),
                              rconst.to_broadcast([P, 2 * E2])),
                             (gsc[:, :], gscale.to_broadcast([P, 2])),
                             (ident_s[:, :], ident), (tri_s[:, :], tri), (iota_s[:, :], iota)):
                sp.dma_start(dst, src).then_inc(in_rc, 16)
            sp.dma_start(gws[:, :, :], gwT).then_inc(in_gw, 16)
            load_up(0, 0, 0)
            load_pair(0, 0, 2)
            with sp.Fori(1, LEAD // 2 - 1) as i:
                load_pair(i * 2, i * 2, i * 2 + 2)
            load_pair(LEAD - 2, LEAD - 2, 0)
            with sp.Fori(LEAD // 2, GLU // 2 - 1) as i:
                load_pair(i * 2, i * 2 - LEAD, i * 2 + (2 - LEAD))
            load_pair(GLU - 2, GLU - 2 - LEAD, None)

            def load_q(e, slot):
                ex_ = slice(e, e + 1) if isinstance(e, int) else bass.ds(e, 1)
                sp.dma_start(raw_q[:, slot, :], wq[ex_].rearrange("a p n -> p (a n)")
                             ).then_inc(q_in[slot], 16)
                for k in range(KT + 1):
                    src = s_up[ex_, k * NG:(k + 1) * NG, :] if k < KT else s_down[ex_]
                    cols = slice(k * P, (k + 1) * P) if k < KT else slice(C, 2 * C)
                    n = src.shape[2]
                    src = src.rearrange("a g n -> (a g) n").unsqueeze(1).to_broadcast([NG, GROUP, n])
                    sp.dma_start(raw_s[:, slot, cols], src
                                 ).then_inc(q_in[slot], 16)
                sp.dma_start(raw_sel[:, slot, :], sel3[ex_].rearrange("a p n -> p (a n)")
                             ).then_inc(q_in[slot], 16)

            load_q(0, 0)
            load_q(1, 1)
            with sp.Fori(1, E3 // 2) as i:
                for slot in range(2):
                    sp.wait_ge(up_hi_ready, i * 2 + (GLU + slot - 1))
                    load_q(i * 2 + slot, slot)
            for n, (hf, m) in enumerate(BLOCKS):
                sp.wait_ge(x_ready, (NL - 1) * len(BLOCKS) + n + 1)
                sp.dma_start(out[m, :, hf * HALF:(hf + 1) * HALF], blk(x, hf, m)).then_inc(out_done, 16)
            sp.wait_ge(out_done, 16 * len(BLOCKS))

        @block.tensor
        def _(pe):
            def split_mm(dst, w_at, rhs_hi, rhs_lo, start, stop):
                n = 0
                for slot, cols, k in w_at:
                    for w, r in ((w_hi, rhs_hi), (w_hi, rhs_lo), (w_lo, rhs_hi)):
                        n += 1
                        mm = pe.matmul(dst, w[:, slot, cols], r(k), start=start and n == 1,
                                       stop=stop and n == 3 * len(w_at), skip_group_check=True)
                return mm

            def up(layer, gs, c, k):
                off, hf = place(layer, k)
                par, slot = k % 2, off % 2
                tok = slice(hf * HALF, (hf + 1) * HALF)

                def col(j):
                    return slice(j * P, (j + 1) * P)

                def hi(kt):
                    return c_hi[:, kt, tok]

                def lo(kt):
                    return c_lo[:, kt, tok]

                if hf == 0 or single(layer, k):
                    pe.wait_ge(up_lo_ready, c + 1)
                if k in firsts(layer):
                    pe.wait_ge(c_lo_ready, 4 * layer + 2 * hf + 2)
                if layer < 3:
                    wait(pe, h_ready, gs - 1)
                elif k < 2:
                    pe.wait_ge(h_ready, S0[3])
                else:
                    pe.wait_ge(act_ready, gs - 1)
                split_mm(g_ps[:, par, :], [(slot, col(j), j) for j in range(KT)], hi, lo,
                         True, True).then_inc(g_ready, 1)
                if layer < 3:
                    wait(pe, t_ready, gs)
                    split_mm(u_ps[:, :], [(slot, col(KT + j), j) for j in range(KT)], hi, lo,
                             True, True).then_inc(u_ready, 1)

            def gate(layer, gs, c, k):
                off, hf = place(layer, k)
                par, slot = k % 2, off % 2
                tok = slice(hf * HALF, (hf + 1) * HALF)
                if k in firsts(layer):
                    pe.wait_ge(gates_ready, 2 * layer + hf + 1)
                wait(pe, act_ready, gs + 1)
                if layer == 3:
                    wait(pe, h_ready, gs)
                pe.matmul(g_ps[:, par, :] if layer < 3 else u_ps[:, :],
                          w_hi[0:KG[layer], slot, UPC:DN0], gates[0:KG[layer], tok],
                          start=True, stop=True, skip_group_check=True).then_inc(gate_ready, 1)

            def down(layer, gs, c, k):
                off, hf = place(layer, k)
                slot, start = off % 2, k in firsts(layer)
                if hf == 0 or single(layer, k):
                    pe.wait_ge(down_lo_ready, c + 1)

                def product(m, w, r, first=False):
                    return pe.matmul(y_ps[:, m, hf, :], w[:, slot, DN0 + m * P:DN0 + (m + 1) * P],
                                     r[:, k % HB, :], start=start and first, stop=False,
                                     skip_group_check=True)

                pe.wait_ge(h_hi_ready, gs + 1)
                for m in range(KT):
                    product(m, w_hi, h_hi, True)
                    product(m, w_lo, h_hi)
                pe.wait_ge(h_lo_ready, gs + 1)
                for m in range(KT):
                    mm = product(m, w_hi, h_lo)
                mm.then_inc(y_done, 1)

            def logits(layer, hf):
                pe.wait_ge(c_ready, 4 * layer + 2 * hf + 2)
                if layer == 0 and hf == 0:
                    pe.wait_ge(in_gw, 16)
                n = GW[layer]
                for i in range(TT)[of_half(hf)]:
                    o = (i % (TT // 2) if layer == 0 else i) * n
                    for kt in range(KT):
                        mm = pe.matmul(y_ps[:, 0, hf if layer == 0 else 0, o:o + n],
                                       cnd[:, kt, i * P:(i + 1) * P],
                                       gws[:, kt, G0[layer]:G0[layer] + n],
                                       start=kt == 0, stop=kt == KT - 1, skip_group_check=True)
                if layer == 0 or hf == 1:
                    mm.then_inc(logits_ready, 1)

            def positions(hf):
                pe.wait_ge(rpe, hf + 1)
                for i in range(TT)[of_half(hf)]:
                    for j in range(i + 1):
                        o = i % (TT // 2) * E0
                        mm = pe.matmul(y_ps[:, 1, hf, o:o + E0], (tri16 if j == i else ones16)[:, :],
                                       sel16[:, j, :], start=j == 0, stop=j == i, skip_group_check=True)
                mm.then_inc(logits_ready, 1)

            def turn0(hf):
                pe.wait_ge(gcat_ready, hf + 1)
                for part, src in enumerate((gcat[:, :, :].bitcast(F32), lg[:, :, :])):
                    for i in range(TT // 2):
                        mm = pe.transpose(y_ps[:, part, hf, i * P:(i + 1) * P],
                                          src[:, hf * (TT // 2) + i, :], ident_s[:, :])
                mm.then_inc(turned, 1)

            def renumber(hf):
                pe.wait_ge(gold_ready, hf * 2 + 2)
                if hf:
                    pe.wait_ge(gates_ready, 1)
                for part in range(2):
                    mm = pe.matmul(r_ps[0:KG[0], :], remap[:, part, :], gold[:, part, :],
                                   start=part == 0, stop=part == 1, skip_group_check=True)
                mm.then_inc(turned, 1)

            def turn(layer):
                pe.wait_ge(gcat_ready, 2 + layer)
                kg = KG[layer]
                for hf, bank in enumerate((r_ps[0:kg, :], y_ps[0:kg, 0, 1, :])):
                    for i in range(TT // 2):
                        mm = pe.transpose(bank[:, i * P:(i + 1) * P],
                                          gcat[:, hf * (TT // 2) + i, 0:kg].bitcast(F32), ident_s[:, :])
                    mm.then_inc(turned, 1)

            pe.wait_ge(in_rc, 7 * 16)
            for layer in range(NL):
                logits(layer, 0)
                up(layer, S0[layer], C0[layer] + place(layer, 0)[0], 0)
                if layer:
                    logits(layer, 1)

                def body(gs, c, k):
                    n = 2 * CH[layer]
                    if k == 0:
                        if layer == 0:
                            positions(0)
                        up(layer, gs + 1, c + 1, 1)
                        if layer == 0:
                            turn0(0)
                            renumber(0)
                        else:
                            if layer == 3:
                                up(layer, gs + 2, C0[3], 2)
                            turn(layer)
                    elif k == LEAD and layer == 0:
                        turn0(1)
                        up(layer, gs, c, k)
                        renumber(1)
                    elif k >= 2 and layer < 3:
                        up(layer, gs, c, k)
                    elif layer == 3 and 2 <= k < n - 1:
                        if k < 4 or k >= n - 5:
                            up(layer, gs + 1, C0[3] + place(3, k + 1)[0], k + 1)
                        else:
                            up(layer, gs + 1, c + k % 2, k + 1)
                    gate(layer, gs, c, k)
                    if k == n - 1 and layer == NL - 1:
                        behind = (k - 2, k - 1, k)
                    elif k >= n - 2 and layer < NL - 1:
                        behind = (k - 2, k - 1) if k == n - 2 else (k - 1, k)
                    else:
                        behind = (k - 2,) if k >= 2 else ()
                    for b in behind:
                        if HEAD[layer] + 4 <= k < n - 4:
                            down(layer, gs - 2, c - 1, b)
                        else:
                            down(layer, gs + (b - k), C0[layer] + place(layer, b)[0], b)
                    if layer == 0 and k == LEAD - 5:
                        logits(0, 1)
                    if layer == 0 and k == LEAD - 2:
                        positions(1)

                steps(pe, layer, body, more=4)

        @block.scalar
        def _(act):
            def up_hi(c, slot, glu):
                if glu:
                    act.wait_ge(raw_up_in[slot], (c - slot) * 8 + 16)
                    act.activation(w_hi[:, slot, 0:DN0], raw[:, slot, 0:DN0], ACT.Copy
                                   ).then_inc(up_hi_ready, 1)
                else:
                    act.wait_ge(w_deq, c - GLU + 1)
                    act.activation(w_hi[:, slot, 0:C], raw[:, slot, 0:C], ACT.Copy)
                    act.activation(w_hi[0:KG[3], slot, UPC:DN0], raw_sel[:, slot, :], ACT.Copy
                                   ).then_inc(up_hi_ready, 1)

            def first_up_hi(layer):
                for slot in range(2):
                    up_hi(C0[layer] + slot, slot, layer < 3)

            def down_hi(slot, c, glu):
                if glu:
                    act.wait_ge(raw_down_in[slot], (c - slot) * 8 + 16)
                act.activation(w_hi[:, slot, DN0:WC], raw[:, slot, DN0:WC], ACT.Copy
                               ).then_inc(down_hi_ready, 1)

            def sigmoid_x(layer, hf):
                for m in range(KT):
                    if layer:
                        act.wait_ge(x_ready, 4 * (layer - 1) + 2 * hf + m + 1)
                    elif hf == m == 0:
                        act.wait_ge(in_x, 16)
                    act.activation(blk(cnd, hf, m), blk(x, hf, m), ACT.Sigmoid).then_inc(sig_ready, 1)

            def split_c(layer, hf):
                for m in range(KT):
                    act.wait_ge(c_ready, 4 * layer + 2 * hf + m + 1)
                    act.activation(blk(c_hi, hf, m), blk(cnd, hf, m), ACT.Copy).then_inc(c_hi_ready, 1)

            def router0_act(hf):
                act.wait_ge(lgt, hf + 1)
                act.activation(ex[:, of_half(hf), :], lg[:, of_half(hf), :], ACT.Exp).then_inc(rexp, 1)

            def router_act(layer):
                n = GW[layer]
                if layer == 2:
                    act.wait_ge(logits_ready, 4 + layer)
                    scores = y_ps[:, 0, 0, 0:TT * n].rearrange("p (i e) -> p i e", i=TT)
                    act.activation(lg[:, :, E2:2 * E2], scores[:, :, E2:2 * E2], ACT.Silu
                                   ).then_inc(rexp, 1)
                    n = E2
                if layer == 3:
                    n = 2 * E3
                act.wait_ge(lgt, 2 + layer)
                act.activation(ex[:, :, 0:n], lg[:, :, 0:n], ACT.Exp).then_inc(rexp, 1)
                if layer == 1:
                    exp_uk(3)

            def gold_copy(hf):
                act.wait_ge(turned, 2 * hf + 1)
                for part in range(2):
                    act.activation(gold[:, part, :], y_ps[:, part, hf, :], ACT.Copy
                                   ).then_inc(gold_ready, 1)

            def gates_copy(layer, hf):
                act.wait_ge(turned, 2 * hf + 2 if layer == 0 else 3 + 2 * layer + hf)
                kg = KG[layer]
                bank = r_ps[0:kg, :] if layer == 0 or hf == 0 else y_ps[0:kg, 0, 1, :]
                act.activation(gates[0:kg, hf * HALF:(hf + 1) * HALF], bank, ACT.Copy
                               ).then_inc(gates_ready, 1)

            def exp_uk(layer, kt=None):
                act.wait_ge(uk_ready, layer + 2)
                q = layer * UNITS + (kt or 0) * NB
                e = R[:, q:q + (UNITS if kt is None else NB), :]
                act.activation(e, e, ACT.Exp).then_inc(euk_ready, 1)

            act.wait_ge(in_wu, 16)
            act.activation(wexp[:, :, :], wus[:, :, 0, :], ACT.Exp).then_inc(act_done, 1)
            act.wait_ge(act_done, 1)
            act.activation(wexp[:, :, :], wexp[:, :, :], ACT.Exp, scale=-1.0).then_inc(wexp_ready, 1)
            act.wait_ge(tf_ready, 1)
            act.activation(tf[:, :], tfs[:, :], ACT.Exp, scale=-1.0).then_inc(tf_ready, 1)
            for hf in range(2):
                act.wait_ge(kmin_ready, hf + 1)
                act.activation(batches(ek, hf), batches(ek, hf), ACT.Exp).then_inc(ek_ready, 1)
                act.wait_ge(ek_ready, hf + 1)
                for kt in range(KT):
                    units = half_units(hf, kt)
                    ins = act.activation(ek_rev[:, units, ::-1], ek[:, units, :], ACT.Copy)
                ins.then_inc(ek_rev_ready, 1)
                act.wait_ge(uk_ready, hf + 1)
                act.activation(batches(R, hf), batches(R, hf), ACT.Exp).then_inc(euk_ready, 1)
            for hf in range(2):
                sigmoid_x(0, hf)
            split_c(0, 0)
            for u in range(2):
                up_hi(u, u, True)
            for layer in range(NL):
                def silu(gs, k):
                    par = k % 2
                    act.wait_ge(g_ready, gs + 1)
                    wait(act, t_ready, gs - 1)
                    act.activation(act_g[:, par, :], g_ps[:, par, :], ACT.Silu if layer < 3 else ACT.Relu
                                   ).then_inc(act_ready, 1)

                if layer:
                    silu(S0[layer], 0)
                    router_act(layer)
                else:
                    exp_uk(1)
                    router0_act(0)
                    silu(0, 0)

                def body(gs, c, k):
                    n = 2 * CH[layer]
                    slot = place(layer, k)[0] % 2
                    regular = HEAD[layer] <= k < (n - 4 if layer < 3 else n)
                    if k > 1 and single(layer, k):
                        act.wait_ge(gate_ready, k)
                        up_hi(k + 1, 1 - slot, True)
                    if k == 0:
                        silu(gs + 1, 1)
                        if layer == 0:
                            gold_copy(0)
                        gates_copy(layer, 0)
                        if layer:
                            gates_copy(layer, 1)
                    elif k == LEAD and layer == 0:
                        gold_copy(1)
                        silu(gs, k)
                        gates_copy(0, 1)
                    elif k > 1 and layer < 3:
                        silu(gs, k)
                    if single(layer, k):
                        if k == 0:
                            act.wait_ge(gate_ready, 1)
                            up_hi(2, 0, True)
                        if k == LEAD - 3:
                            router0_act(1)
                        if k in (LEAD + 1, LEAD + 3):
                            exp_uk(2, (k - LEAD) // 2)
                    elif k == 1 or k == 2:
                        if k == 1:
                            act.wait_ge(y_done, S0[layer])
                        down_hi(k - 1, C0[layer] + k - 1, layer < 3)
                        if k == 2 and layer == 3:
                            act.wait_ge(gate_ready, gs + 1)
                            up_hi(C0[layer] + 2, 0, False)
                    elif k == 3:
                        if layer < 3:
                            act.wait_ge(gate_ready, gs)
                            up_hi(C0[layer] + 2, 0, True)
                    elif (k == n - 4 and layer < 3) or (regular and k % 2 == 0 and k < n - 2):
                        act.wait_ge(gate_ready, gs)
                        up_hi(c + 1, 1 - slot, layer < 3)
                    elif (k in (n - 3, n - 2) and layer < 3) or (regular and k % 2):
                        act.wait_ge(y_done, gs - 2)
                        if regular:
                            down_hi(slot, c, layer < 3)
                        else:
                            down_hi(k - (n - 3), C0[layer + 1] - 2 + k - (n - 3), True)
                    elif k == n - 1 and layer < NL - 1:
                        sigmoid_x(layer + 1, 0)
                    if layer == 3 and 0 < k < n - 1:
                        silu(gs + 1, k + 1)
                    act.wait_ge(h_ready, gs + 1)
                    wait(act, y_done, gs - 3)
                    act.activation(h_hi[:, k % HB, :], h[:, k % 2, :], ACT.Copy).then_inc(h_hi_ready, 1)
                    if single(layer, k):
                        wait(act, y_done, k - 1)
                        down_hi(slot, k, True)
                        if k == LEAD - 5:
                            split_c(0, 1)
                    if k == n - 1 and layer < NL - 1:
                        split_c(layer + 1, 0)
                        act.wait_ge(gate_ready, gs + 1)
                        first_up_hi(layer + 1)

                steps(act, layer, body)
                if layer < NL - 1:
                    sigmoid_x(layer + 1, 1)
                    split_c(layer + 1, 1)

        @block.vector
        def _(dve):
            count = [0]

            def link(ins):
                count[0] += 1
                ins.then_inc(dve_done, 1)
                dve.wait_ge(dve_done, count[0])

            def scans(q, src_q, buf):
                dec = decay[:, bass.ds(q, 1)].to_broadcast([P, NT])
                for n, (src, rev) in enumerate(((ekv, ekv_rev), (ek, ek_rev))):
                    dve.tensor_tensor_scan(fwd[:, buf, n, :], dec, unit(src, src_q), 0.0, ALU.mult, ALU.add)
                    last = dve.tensor_tensor_scan(bwd[:, buf, n, ::-1], dec, unit(rev, src_q), 0.0,
                                                  ALU.mult, ALU.add)
                last.then_inc(scan_ready, 1)

            def invert(o, buf):
                dve.wait_ge(num_ready, o + 1)
                den = fwd[:, buf, 1, :]
                dve.tensor_scalar(den, den, 1e-8, None, ALU.max).then_inc(R_ready, 1)
                dve.wait_ge(R_ready, o * 3 + 1)
                dve.reciprocal(den, den).then_inc(R_ready, 1)

            def ratio(o, q, buf):
                dve.wait_ge(R_ready, o * 3 + 2)
                dve.scalar_tensor_tensor(out=unit(R, q), in0=fwd[:, buf, 0, :],
                                         scalar=oscale[:, bass.ds(q, 1)], in1=fwd[:, buf, 1, :],
                                         op0=ALU.mult, op1=ALU.mult).then_inc(R_ready, 1)
                dve.wait_ge(R_ready, o * 3 + 3)

            dve.wait_ge(in_te, 16)
            dve.tensor_reduce(tfs[:, :], te[:, :, :], AX, ALU.add).then_inc(tf_ready, 1)
            dve.wait_ge(in_fs[0], 16)
            dve.tensor_scalar(batches(ek, 0), batches(fs, 0), 30.0, None, ALU.min).then_inc(kmin_ready, 1)
            dve.wait_ge(in_wu, 16)

            def add_u(layer):
                for kt in range(KT):
                    q = layer * UNITS + kt * NB
                    ins = dve.tensor_scalar(R[:, q:q + NB, :], fs[:, kt * NB:(kt + 1) * NB, :],
                                            wus[:, layer, 1, kt:kt + 1], 30.0, ALU.add, ALU.min)
                ins.then_inc(uk_ready, 1)

            def add_u0(hf):
                for kt in range(KT):
                    units = half_units(hf, kt)
                    ins = dve.tensor_scalar(R[:, units, :], fs[:, units, :], wus[:, 0, 1, kt:kt + 1], 30.0,
                                            ALU.add, ALU.min)
                ins.then_inc(uk_ready, 1)

            def weigh(hf):
                dve.wait_ge(ek_ready, hf + 1)
                link(dve.tensor_tensor(batches(ekv, hf), batches(ek, hf), batches(fs, hf), ALU.mult))
                for kt in range(KT):
                    units = half_units(hf, kt)
                    ins = dve.tensor_copy(ekv_rev[:, units, ::-1], ekv[:, units, :])
                link(ins)
                dve.wait_ge(ek_rev_ready, hf + 1)

            add_u0(0)
            dve.wait_ge(tf_ready, 2)
            link(dve.tensor_scalar(tf[:, :], tf[:, :], 1.0, None, ALU.add))
            link(dve.reciprocal(tf[:, :], tf[:, :]))
            link(dve.tensor_scalar(tdec[:, :], tf[:, :], 0.5, 0.5, ALU.mult, ALU.add))
            dve.wait_ge(wexp_ready, 1)
            shape = [P, NL * KT, NB]
            dve.tensor_tensor(decay[:, :].rearrange("p (a b) -> p a b", b=NB),
                              tdec[:, :].unsqueeze(1).to_broadcast(shape),
                              wexp[:, :, :].rearrange("p l k -> p (l k)").unsqueeze(2).to_broadcast(shape),
                              ALU.mult)
            link(dve.tensor_scalar(oscale[:, :].rearrange("p (a b) -> p a b", b=NB),
                                   tf[:, :].unsqueeze(1).to_broadcast(shape), 0.2, 0.8,
                                   ALU.mult, ALU.add))
            weigh(0)
            def scans0(o):
                scans(UNIT0[o], UNIT0[o], o % 2)

            def finish0(o):
                invert(o, o % 2)
                ratio(o, UNIT0[o], o % 2)

            def router0_tables():
                dve.wait_ge(in_rc, 7 * 16)
                dve.tensor_copy(tri16[:, :], tri_s[:, :])
                dve.memset(ones16[:, :], 1.0)
                dve.tensor_copy(o2n_c[:, :], o2n_ci[:, :])
                link(dve.tensor_copy(keep[:, 0, :], keep_i[:, :]))
                link(dve.tensor_scalar(keep[:, 0, :], keep[:, 0, :], -1.0, None, ALU.not_equal))
                dve.tensor_scalar(keep[:, 1, :], keep[:, 0, :], -1.0, 1e30, ALU.add, ALU.mult)
                for part in range(2):
                    link(dve.memset(remap[:, part, :].bitcast(F32), 0.0))
                    link(dve.tensor_scalar(remap[:, part, part * KEPT:(part + 1) * KEPT],
                                           iota_s[:, 0:KEPT], o2n_c[:, 0:1], None, ALU.is_equal))

            scans0(0)
            for o in range(UNITS // 2 - 1):
                scans0(o + 1)
                if o == 0:
                    dve.wait_ge(in_fs[1], 16)
                    dve.tensor_scalar(batches(ek, 1), batches(fs, 1), 30.0, None, ALU.min
                                      ).then_inc(kmin_ready, 1)
                    add_u0(1)
                if o == 1:
                    router0_tables()
                finish0(o)
            finish0(UNITS // 2 - 1)

            def cond(layer, hf):
                for m in range(KT):
                    dve.wait_ge(sig_ready, 4 * layer + 2 * hf + m + 1)
                    q = layer * UNITS + m * NB + hf * NB // 2
                    dve.tensor_tensor(blk(cnd, hf, m), blk(cnd, hf, m),
                                      R[:, q:q + NB // 2, :].rearrange("p a n -> p (a n)"), ALU.mult
                                      ).then_inc(c_ready, 1)

            def spread(v, n):
                return v.unsqueeze(2).to_broadcast([P, TT, n])

            def add_y(layer, hf):
                last = max(k for k in range(2 * CH[layer]) if place(layer, k)[1] == hf)
                dve.wait_ge(y_done, S0[layer] + last + 1)
                for m in range(KT):
                    dve.tensor_tensor(blk(x, hf, m), blk(x, hf, m), y_ps[:, m, hf, :], ALU.add
                                      ).then_inc(x_ready, 1)

            def product(layer, gs, k):
                par = k % 2
                dve.wait_ge(act_ready, gs + 1)
                if layer < 3:
                    dve.wait_ge(u_ready, gs + 1)
                other = u_ps[:, :] if layer < 3 else act_g[:, par, :]
                dve.tensor_tensor(t[:, par, :], act_g[:, par, :], other, ALU.mult).then_inc(t_ready, 1)

            def softmax_parts(layer, src, n):
                link(dve.tensor_reduce(r8[:, 0, :], src, AX, ALU.max))
                dve.tensor_tensor(lg[:, :, 0:n], src, spread(r8[:, 0, :], n), ALU.subtract
                                  ).then_inc(lgt, 1)
                dve.wait_ge(rexp, [0, 3, 5, 6][layer])
                ins = dve.tensor_reduce(r8[:, 1, :], ex[:, :, 0:n], AX, ALU.add)
                if layer == 2:
                    link(ins)

            def top2(src, n, low):
                for i in range(TT):
                    ins = dve.max(v8[:, i, :], src[:, i, 0:n])
                link(ins)
                link(dve.memset(v8[:, :, 2:8], 2 * low))
                for i in range(TT):
                    ins = dve.match_replace(top[:, i, 0:n], v8[:, i, :], src[:, i, 0:n], low)
                link(ins)

            def chosen(dst, src, n, low):
                link(dve.scalar_tensor_tensor(out=dst, in0=top[:, :, 0:n], scalar=low,
                                              in1=src, op0=ALU.is_equal, op1=ALU.mult))

            def parts(g, n, one):
                n += one
                link(dve.tensor_copy(gcat[:, :, 0:n], g[:, :, 0:n]))
                dve.tensor_tensor(gcat[:, :, n:2 * n], g[:, :, 0:n], gcat[:, :, 0:n].bitcast(F32),
                                  ALU.subtract).then_inc(gcat_ready, 1)

            def magnitude(dst, src):
                return dve.scalar_tensor_tensor(out=dst, in0=src, scalar=-1.0, in1=src, op0=ALU.mult,
                                                op1=ALU.max)

            def router0_start(hf):
                half = of_half(hf)
                dve.wait_ge(logits_ready, 2 * hf + 1)
                yl = y_ps[:, 0, hf, :].rearrange("p (i e) -> p i e", e=E0)
                link(dve.tensor_tensor(lg[:, half, :], yl,
                                       keep[:, 1:2, :].to_broadcast([P, TT // 2, E0]), ALU.add))
                link(dve.tensor_reduce(r8[:, 0, half], lg[:, half, :], AX, ALU.max))
                dve.tensor_tensor(lg[:, half, :], lg[:, half, :],
                                  r8[:, 0, half].unsqueeze(2).to_broadcast([P, TT // 2, E0]),
                                  ALU.subtract).then_inc(lgt, 1)

            def router0_choose(hf):
                half = of_half(hf)
                dve.wait_ge(rexp, hf + 1)
                for i in range(TT)[half]:
                    ins = dve.max(v8[:, i, :], ex[:, i, :])
                link(ins)
                for i in range(TT)[half]:
                    ins = dve.match_replace(lg[:, i, :], v8[:, i, :], ex[:, i, :], -1.0)
                link(ins)
                l, e = lg[:, half, :], ex[:, half, :]
                dve.tensor_scalar(sel16[:, half, :], l, 0.0, None, ALU.is_lt).then_inc(rpe, 1)
                if hf == 0:
                    product(0, 0, 0)
                link(dve.scalar_tensor_tensor(out=e, in0=l, scalar=0.0, in1=e, op0=ALU.is_lt,
                                              op1=ALU.mult))
                link(dve.tensor_reduce(r8[:, 2, half], v8[:, half, :], AX, ALU.add))
                link(dve.reciprocal(r8[:, 3, half], r8[:, 2, half]))
                link(dve.tensor_tensor(e, e, r8[:, 3, half].unsqueeze(2).to_broadcast([P, TT // 2, E0]),
                                       ALU.mult))

            def router0_cap(hf):
                half = of_half(hf)
                l, e = lg[:, half, :], ex[:, half, :]
                dve.wait_ge(logits_ready, 2 + 2 * hf)
                yp = y_ps[:, 1, hf, :].rearrange("p (i e) -> p i e", e=E0)
                link(dve.scalar_tensor_tensor(out=e, in0=yp, scalar=CAP - 0.5, in1=e,
                                              op0=ALU.is_lt, op1=ALU.mult))
                link(dve.tensor_copy(gcat[:, half, :], e))
                dve.tensor_tensor(l, e, gcat[:, half, :].bitcast(F32), ALU.subtract
                                  ).then_inc(gcat_ready, 1)

            def router(layer):
                n = [E0, E1, E2, E3][layer]
                rp = y_ps[:, 0, 0, 0:TT * GW[layer]].rearrange("p (i e) -> p i e", i=TT)
                dve.wait_ge(logits_ready, 4 + layer)
                if layer < 3:
                    dve.memset(ex[:, :, n:n + 1], 1.0)
                if layer == 1:
                    softmax_parts(1, rp, n)
                    top2(ex, n, -1.0)
                elif layer == 2:
                    dve.wait_ge(rexp, 4)
                    link(dve.tensor_tensor(lg[:, :, 0:n], rp[:, :, 0:n], lg[:, :, E2:2 * E2], ALU.mult))
                    link(magnitude(lg[:, :, 0:n], lg[:, :, 0:n]))
                    softmax_parts(2, lg[:, :, 0:n], n)
                    link(dve.reciprocal(r8[:, 3, :], r8[:, 1, :]))
                    link(dve.tensor_tensor(ex[:, :, 0:n], ex[:, :, 0:n], spread(r8[:, 3, :], n), ALU.mult))
                    link(dve.tensor_tensor(lg[:, :, 0:n], ex[:, :, 0:n],
                                           rcs[:, 1:2, :].to_broadcast([P, TT, n]), ALU.add))
                    top2(lg, n, -1e30)
                    link(dve.tensor_tensor(ex[:, :, 0:n], ex[:, :, 0:n],
                                           rcs[:, 0:1, :].to_broadcast([P, TT, n]), ALU.mult))
                    link(dve.tensor_scalar(ex[:, :, 0:n], ex[:, :, 0:n], 1.0, None, ALU.add))
                    chosen(ex[:, :, 0:n], ex[:, :, 0:n], n, -1e30)
                    parts(ex, n, True)
                    return
                else:
                    a, b, z = (lg[:, :, j * n:(j + 1) * n] for j in range(3))
                    dve.tensor_scalar(a, rp, 0.0, None, ALU.min)
                    link(dve.tensor_copy(z, rp))
                    dve.scalar_tensor_tensor(out=b, in0=z, scalar=-1.0, in1=z, op0=ALU.mult, op1=ALU.min)
                    link(dve.tensor_reduce(r8[:, 0, :], a, AX, ALU.max))
                    dve.tensor_tensor(a, a, spread(r8[:, 0, :], n), ALU.subtract).then_inc(lgt, 1)
                    dve.wait_ge(rexp, 6)
                    link(dve.tensor_scalar(ex[:, :, n:2 * n], ex[:, :, n:2 * n], 1.0, None, ALU.add))
                    link(dve.reciprocal(ex[:, :, n:2 * n], ex[:, :, n:2 * n]))
                    link(dve.tensor_tensor(ex[:, :, 0:n], ex[:, :, 0:n], ex[:, :, n:2 * n], ALU.mult))
                    dve.tensor_reduce(r8[:, 1, :], ex[:, :, 0:n], AX, ALU.add)
                    top2(ex, n, -1.0)
                chosen(ex[:, :, 0:n], ex[:, :, 0:n], n, -1.0)
                link(dve.tensor_reduce(r8[:, 2, :], ex[:, :, 0:n], AX, ALU.add))
                link(dve.scalar_tensor_tensor(out=r8[:, 2, :], in0=r8[:, 1, :], scalar=EPS,
                                              in1=r8[:, 2, :], op0=ALU.mult, op1=ALU.add))
                link(dve.reciprocal(r8[:, 3, :], r8[:, 2, :]))
                link(dve.tensor_tensor(ex[:, :, 0:n], ex[:, :, 0:n], spread(r8[:, 3, :], n), ALU.mult))
                parts(ex, n, layer == 1)

            def dequantize(e, slot):
                dve.wait_ge(q_in[slot], (e - slot) * (8 * QLOADS) + 16 * QLOADS)
                dve.wait_ge(down_lo_ready, e + (GLU - 1))
                up, dn = raw[:, slot, 0:C], raw[:, slot, DN0:WC]
                dve.scalar_tensor_tensor(out=up, in0=raw_q[:, slot, 0:C], scalar=-8.0,
                                         in1=raw_s[:, slot, 0:C], op0=ALU.add, op1=ALU.mult)
                dve.scalar_tensor_tensor(out=dn, in0=raw_q[:, slot, C:2 * C], scalar=-8.0,
                                         in1=raw_s[:, slot, C:2 * C], op0=ALU.add, op1=ALU.mult
                                         ).then_inc(w_deq_part, 1)
                dve.wait_ge(w_deq_part, e * 2 + 1)
                dve.tensor_scalar(up, up, gsc[:, 0:1], None, ALU.mult).then_inc(w_deq_part, 1)
                dve.tensor_scalar(dn, dn, gsc[:, 1:2], None, ALU.mult).then_inc(w_deq, 1)

            def weights_lo(slot, cols, hi_sem, lo_sem, c):
                dve.wait_ge(hi_sem, c + 1)
                dve.tensor_tensor(w_lo[:, slot, cols], raw[:, slot, cols],
                                  w_hi[:, slot, cols].bitcast(F32), ALU.subtract).then_inc(lo_sem, 1)

            def wkv(q, k):
                if k == 0:
                    scans(q, q % UNITS, 0)
                if k == 2:
                    invert(q, 0)
                if k == 3:
                    ratio(q, q, 0)

            def up_lo(c, slot, glu):
                weights_lo(slot, slice(0, UPC if glu else C), up_hi_ready, up_lo_ready, c)

            def down_lo(c, slot):
                weights_lo(slot, slice(DN0, WC), down_hi_ready, down_lo_ready, c)

            def first_up_lo(layer):
                for slot in range(2):
                    up_lo(C0[layer] + slot, slot, layer < 3)

            cond(0, 0)
            weigh(1)
            for u in range(2):
                up_lo(u, u, True)

            for layer in range(NL):
                if layer == 0:
                    add_u(1)
                    router0_start(0)
                    scans0(4)
                    router0_choose(0)
                    router0_cap(0)
                    scans0(5)
                    finish0(4)
                else:
                    product(layer, S0[layer], 0)
                    router(layer)

                def body(gs, c, k):
                    n = 2 * CH[layer]
                    par, slot = k % 2, place(layer, k)[0] % 2
                    if k == n - 1 and layer < 3:
                        add_y(layer, 0)
                    if k and single(layer, k):
                        up_lo(k + 1, 1 - slot, True)
                    if k > 0:
                        product(layer, gs, k)
                    regular = HEAD[layer] <= k < (n - 4 if layer < 3 else n)
                    next_up = regular and not par and k < n - 2
                    if next_up and layer == 3:
                        up_lo(c + 1, 1 - slot, False)
                    dve.wait_ge(t_ready, gs + 1)
                    dve.wait_ge(gate_ready, gs + 1)
                    wait(dve, h_lo_ready, gs - 1)
                    gate_ps = g_ps[:, par, :] if layer < 3 else u_ps[:, :]
                    dve.tensor_tensor(h[:, par, :], t[:, par, :], gate_ps, ALU.mult).then_inc(h_ready, 1)
                    if single(layer, k):
                        if k:
                            down_lo(k - 1, 1 - slot)
                        if k == 2 * LEAD - 1:
                            down_lo(k, slot)
                        if k in (1, 2):
                            scans0(5 + k)
                        if k in (1, 2, 3):
                            finish0(4 + k)
                        if k == LEAD - 6:
                            cond(0, 1)
                        if k == LEAD - 4:
                            router0_start(1)
                        if k == LEAD - 3:
                            router0_choose(1)
                        if k == LEAD - 2:
                            router0_cap(1)
                        if k in (LEAD, LEAD + 4):
                            add_u(2 + (k - LEAD) // 4)
                    elif k in (3, n - 4) and layer < 3:
                        up_lo(c + 1, 1 - slot, True)
                    elif k == 3:
                        dequantize(3, 1)
                    elif next_up and layer < 3:
                        up_lo(c + 1, 1 - slot, True)
                    elif k in (1, 2):
                        if k == 2 and layer == 3:
                            up_lo(C0[layer] + 2, 0, False)
                        down_lo(C0[layer] + k - 1, k - 1)
                        if layer == 3 and k == 1:
                            dequantize(2, 0)
                    elif regular and par:
                        down_lo(c, slot)
                        if layer == 3 and k < n - 4:
                            dequantize(c + (2 - GLU), slot)
                    elif k in (n - 3, n - 2) and layer < 3:
                        s_dn = k - (n - 3)
                        down_lo(C0[layer] + CH[layer] - 2 + s_dn, s_dn)
                        if layer == 2:
                            dequantize(s_dn, s_dn)
                    elif k == n - 1 and layer < NL - 1:
                        cond(layer + 1, 0)
                    if k == n - 1 and layer == 3:
                        add_y(layer, 0)

                steps(dve, layer, body, wkv)
                if layer < NL - 1:
                    first_up_lo(layer + 1)
                add_y(layer, 1)
                if layer < NL - 1:
                    cond(layer + 1, 1)

        @block.gpsimd
        def _(pool):
            def lo_part(dst, src, hi):
                return pool.tensor_tensor(dst, src, hi.bitcast(F32), ALU.subtract)

            def wkv_dif(o, q, src_q, buf):
                e, dv, d = unit(R, q), dif[:, buf, 0, :], dif[:, buf, 1, :]
                pool.tensor_tensor(d, e, unit(ek, src_q), ALU.subtract).then_inc(dif_ready, 1)
                pool.wait_ge(dif_ready, o * 2 + 1)
                pool.tensor_tensor(dv, d, unit(fs, src_q), ALU.mult).then_inc(dif_ready, 1)

            def wkv_sum(o, buf):
                pool.wait_ge(scan_ready, o + 1)
                pool.wait_ge(dif_ready, o * 2 + 2)
                s = fwd[:, buf, :, :].rearrange("p f n -> p (f n)")
                pool.tensor_tensor(s, s, bwd[:, buf, :, :].rearrange("p f n -> p (f n)"), ALU.add
                                   ).then_inc(sum_ready, 1)
                pool.wait_ge(sum_ready, o + 1)
                pool.tensor_tensor(s, s, dif[:, buf, :, :].rearrange("p f n -> p (f n)"), ALU.add
                                   ).then_inc(num_ready, 1)

            def dif0(o):
                if o == UNITS // 2:
                    pool.wait_ge(euk_ready, 2)
                if o >= 2:
                    pool.wait_ge(num_ready, o - 1)
                wkv_dif(o, UNIT0[o], UNIT0[o], o % 2)

            def sum0(o):
                wkv_sum(o, o % 2)

            def wkv(q, k):
                if k == 0:
                    wkv_dif(q, q, q % UNITS, 0)
                if k == 1:
                    wkv_sum(q, 0)

            def split_c(layer, hf):
                for m in range(KT):
                    pool.wait_ge(c_hi_ready, 4 * layer + 2 * hf + m + 1)
                    lo_part(blk(c_lo, hf, m), blk(cnd, hf, m), blk(c_hi, hf, m)).then_inc(c_lo_ready, 1)

            pool.wait_ge(euk_ready, 1)
            dif0(0)
            dif0(1)
            for o in range(UNITS // 2):
                sum0(o)
                if o < 2:
                    dif0(o + 2)
            for layer in range(NL):
                split_c(layer, 0)
                if layer:
                    split_c(layer, 1)
                    if layer == 1:
                        pool.wait_ge(euk_ready, 4 + KT)
                else:
                    dif0(4)
                    dif0(5)
                    sum0(4)
                    dif0(6)
                    sum0(5)

                def body(gs, c, k):
                    pool.wait_ge(h_hi_ready, gs + 1)
                    lo_part(h_lo[:, k % HB, :], h[:, k % 2, :], h_hi[:, k % HB, :]).then_inc(h_lo_ready, 1)
                    if single(layer, k):
                        if k in (1, 2):
                            sum0(5 + k)
                        if k == 1:
                            dif0(7)
                        if k == LEAD - 5:
                            split_c(0, 1)
                        if k == 2 * LEAD - 1:
                            pool.wait_ge(euk_ready, 3 + KT)

                steps(pool, layer, body, wkv)


def constants():
    import numpy as np
    sels = []
    for n_exp, inter, shared, chunks in ((KEPT, I0, 0, CH[0]), (E1, I1, SH1, CH[1]), (E2, I2, SH2, CH[2])):
        rows = n_exp + (shared > 0)
        s = np.zeros((P, chunks * P), np.float32)
        for e in range(n_exp + (shared > 0)):
            cols = slice(e * inter, (e + 1) * inter) if e < n_exp else slice(e * inter, e * inter + shared)
            s[e, cols] = 1.0
            s[rows + e, cols] = 1.0
        sels.append(s.reshape(P, chunks, P).transpose(1, 0, 2))
    sel3 = np.zeros((E3, KG[3], P), np.float32)
    for e in range(E3):
        sel3[e, [e, E3 + e], :] = 1.0
    tri = np.triu(np.ones((P, P), np.float32), 1)
    iota = np.tile(np.arange(E0, dtype=np.float32), (P, 1))
    return sels, sel3, np.eye(P, dtype=np.float32), tri, iota


def pack_glu(gate, up, down, sel, chunks):
    import numpy as np
    pad = chunks * P - gate.shape[1]
    gate, up = (np.pad(a, ((0, 0), (0, pad))) for a in (gate, up))
    down = np.pad(down, ((0, pad), (0, 0)))
    gu = [a.reshape(KT, P, chunks, P).transpose(2, 1, 0, 3).reshape(chunks, P, KT * P) for a in (gate, up)]
    return np.concatenate(gu + [sel, down.reshape(chunks, P, C)], axis=2)


def kernel(**inputs):
    import numpy as np
    import concourse.bacc as bacc
    from concourse import mybir as _mybir
    from concourse.bass_utils import run_bass_kernel_spmd

    a = {k: np.asarray(v) for k, v in inputs.items()}
    sels, sel3, ident, tri, iota = constants()

    def rows(w):
        return w.reshape(-1, C).T

    def cols(w):
        return w.transpose(0, 2, 1).reshape(-1, C)

    gu = a["L0_ffn_gate_up_proj"]
    packs = [pack_glu(rows(gu[:, :I0]), rows(gu[:, I0:]), cols(a["L0_ffn_down_proj"]), sels[0], CH[0])]
    flat = {n: a["L1_ffn_" + n].transpose(1, 0, 2).reshape(C, -1) for n in ("wg", "wu")}
    packs.append(pack_glu(np.concatenate([flat["wg"], a["L1_ffn_sg"]], 1),
                          np.concatenate([flat["wu"], a["L1_ffn_su"]], 1),
                          np.concatenate([a["L1_ffn_wd"].reshape(-1, C), a["L1_ffn_sd"]], 0), sels[1], CH[1]))
    packs.append(pack_glu(np.concatenate([rows(a["L2_ffn_wg"]), rows(a["L2_ffn_sg"])], 1),
                          np.concatenate([rows(a["L2_ffn_wu"]), rows(a["L2_ffn_su"])], 1),
                          np.concatenate([cols(a["L2_ffn_wd"]), a["L2_ffn_sd"].T], 0), sels[2], CH[2]))
    up_q = a["L3_ffn_fc_up_qweights"].reshape(E3, KT, P, I3).transpose(0, 2, 1, 3).reshape(E3, P, C)
    gw = np.concatenate([a["L0_ffn_gate_weight"], a["L1_ffn_router_w"], a["L2_ffn_cls_w"],
                         a["L2_ffn_gate_w"], a["L3_ffn_gate_weight"]], 0)
    wu = np.stack([np.stack([a[f"L{l}_cond_{n}"] for n in "wu"]) for l in range(NL)])
    arrays = {
        "xT": a["x"].reshape(TOK, C).T.reshape(KT, P, TOK),
        "fT": a["fside_BxSxS_0"].reshape(TOK, C).T.reshape(KT, P, TOK),
        "cond": a["cond_512"].reshape(1, NB * TD),
        "wu": wu.reshape(NL * 2 * KT, P).T,
        "o2n_row": a["L0_ffn_old_to_new"].reshape(1, E0),
        "o2n_col": a["L0_ffn_old_to_new"].reshape(E0, 1),
        "gwT": gw.T.reshape(KT, P, -1).transpose(1, 0, 2),
        "rconst": np.concatenate([a["L2_ffn_extra_scale"], a["L2_ffn_extra_bias"]]).reshape(1, -1),
        "gscale": np.concatenate([a["L3_ffn_fc_up_global_scale"],
                                  a["L3_ffn_fc_down_global_scale"]]).reshape(1, 2),
        "wglu": np.concatenate(packs, 0),
        "wq": np.concatenate([up_q, a["L3_ffn_fc_down_qweights"]], 2),
        "s_up": a["L3_ffn_fc_up_blocks_scale"],
        "s_down": a["L3_ffn_fc_down_blocks_scale"],
        "sel3": sel3, "ident": ident, "tri": tri, "iota": iota,
    }
    nc = bacc.Bacc("TRN2", target_bir_lowering=False, num_devices=1)
    arrays = {f"in_{k}": np.ascontiguousarray(v) for k, v in arrays.items()}
    aps = [nc.dram_tensor(k, v.shape, _mybir.dt.from_np(v.dtype), kind="ExternalInput").ap()
           for k, v in arrays.items()]
    out = nc.dram_tensor("out", (KT, P, TOK), F32, kind="ExternalOutput").ap()
    build(nc, *aps, out)
    r = run_bass_kernel_spmd(nc, [arrays], core_ids=[0])
    return r.results[0]["out"].reshape(C, TOK).T.reshape(NB, NT, C)
```
